# Optimizing a Trainium2 kernel written in Bass

```python
import numpy as np
import jax
import jax.numpy as jnp

def _softmax(x, axis=-1):
    return jax.nn.softmax(x, axis=axis)

def _gelu(x):
    return jax.nn.gelu(x, approximate=True)

def _silu(x):
    return jax.nn.silu(x)

def _sigmoid(x):
    return jax.nn.sigmoid(x)

def _layernorm(x, axis=-1, eps=1e-05):
    m = jnp.mean(x, axis=axis, keepdims=True)
    v = jnp.var(x, axis=axis, keepdims=True)
    return (x - m) / jnp.sqrt(v + eps)

def _scatter_add(tgt, idx, src, axis=0):
    return tgt.at[idx].add(src)

def _segment_sum(src, seg, n):
    return jax.ops.segment_sum(src, seg, n)
kernel_name = 'mk_conv_seq_d2_conv_nchw1024_r2_ce673d'

def setup_inputs(seed: int=0):
    np.random.seed(seed)
    _w = jnp.asarray

    def _rec_inputs():
        import jax
        import jax.numpy as jnp
        _gk = jax.random.key(seed)
        x = -0.0003957 + 1 * jax.random.normal(jax.random.fold_in(_gk, 1), (32, 512, 14, 14), jnp.float32)
        return x
    x = _rec_inputs()

    def _L0_conv_setup():
        import jax, jax.numpy as jnp
        import numpy as np
        EPS = 1e-05

        def _conv(x, w, b, stride, pad):
            y = jax.lax.conv_general_dilated(x, w, window_strides=(stride, stride), padding=[(pad, pad), (pad, pad)], dimension_numbers=('NCHW', 'OIHW', 'NCHW'))
            return y + b.reshape(1, -1, 1, 1)

        def _bn(x, gamma, beta):
            mean = jnp.mean(x, axis=(0, 2, 3), keepdims=True)
            var = jnp.var(x, axis=(0, 2, 3), keepdims=True)
            xn = (x - mean) * jax.lax.rsqrt(var + EPS)
            return gamma.reshape(1, -1, 1, 1) * xn + beta.reshape(1, -1, 1, 1)
        key = jax.random.key(seed)
        ks = jax.random.split(key, 8)
        N, Cin, H, W = (32, 512, 14, 14)
        P = 128
        Cout = P * 4

        def kaiming(k, shape):
            fan_in = shape[1] * shape[2] * shape[3]
            return jax.random.normal(k, shape, jnp.float32) * np.float32(np.sqrt(2.0 / fan_in))
        return {'x': jax.random.normal(ks[0], (N, Cin, H, W), jnp.float32), 'w1': kaiming(ks[1], (P, Cin, 1, 1)), 'b1': jnp.zeros((P,), jnp.float32), 'g1': jnp.ones((P,), jnp.float32), 'be1': jnp.zeros((P,), jnp.float32), 'w2': kaiming(ks[2], (P, P, 3, 3)), 'b2': jnp.zeros((P,), jnp.float32), 'g2': jnp.ones((P,), jnp.float32), 'be2': jnp.zeros((P,), jnp.float32), 'w3': kaiming(ks[3], (Cout, P, 1, 1)), 'b3': jnp.zeros((Cout,), jnp.float32), 'g3': jnp.ones((Cout,), jnp.float32), 'be3': jnp.zeros((Cout,), jnp.float32), 'residual_scale': jnp.zeros((1,), jnp.float32)}
    _L0_conv_all = _L0_conv_setup()
    _L0_conv_in = {k: v for k, v in _L0_conv_all.items() if k in ('w1', 'b1', 'g1', 'be1', 'w2', 'b2', 'g2', 'be2', 'w3', 'b3', 'g3', 'be3', 'residual_scale')}
    del _L0_conv_all

    def _L1_conv_setup():
        import jax, jax.numpy as jnp
        import numpy as np

        def _conv(x, w, padding):
            return jax.lax.conv_general_dilated(x, w, window_strides=(1, 1), padding=padding, dimension_numbers=('NCHW', 'OIHW', 'NCHW'))
        key = jax.random.key(seed)
        ks = jax.random.split(key, 4)
        B, Cin, H, W = (64, 512, 14, 14)
        planes, expansion = (128, 4)
        x = jax.random.normal(ks[0], (B, Cin, H, W), dtype=jnp.float32)
        w1 = jax.random.normal(ks[1], (planes, Cin, 1, 1), dtype=jnp.float32) * 0.02
        w2 = jax.random.normal(ks[2], (planes, planes, 3, 3), dtype=jnp.float32) * 0.02
        w3 = jax.random.normal(ks[3], (planes * expansion, planes, 1, 1), dtype=jnp.float32) * 0.02
        z = jnp.zeros((1,), dtype=jnp.float32)
        return {'x': x, 'w1': w1, 'w2': w2, 'w3': w3, 'bias1b': z, 'bias2a': z, 'bias2b': z, 'bias3a': z, 'bias3b': z, 'rscale': jnp.ones((1,), dtype=jnp.float32), 'rbias': z}
    _L1_conv_all = _L1_conv_setup()
    _L1_conv_in = {k: v for k, v in _L1_conv_all.items() if k in ('w1', 'w2', 'w3', 'bias1b', 'bias2a', 'bias2b', 'bias3a', 'bias3b', 'rscale', 'rbias')}
    del _L1_conv_all
    return {'x': x, 'L0_conv_w1': _L0_conv_in['w1'], 'L0_conv_b1': _L0_conv_in['b1'], 'L0_conv_g1': _L0_conv_in['g1'], 'L0_conv_be1': _L0_conv_in['be1'], 'L0_conv_w2': _L0_conv_in['w2'], 'L0_conv_b2': _L0_conv_in['b2'], 'L0_conv_g2': _L0_conv_in['g2'], 'L0_conv_be2': _L0_conv_in['be2'], 'L0_conv_w3': _L0_conv_in['w3'], 'L0_conv_b3': _L0_conv_in['b3'], 'L0_conv_g3': _L0_conv_in['g3'], 'L0_conv_be3': _L0_conv_in['be3'], 'L0_conv_residual_scale': _L0_conv_in['residual_scale'], 'L1_conv_w1': _L1_conv_in['w1'], 'L1_conv_w2': _L1_conv_in['w2'], 'L1_conv_w3': _L1_conv_in['w3'], 'L1_conv_bias1b': _L1_conv_in['bias1b'], 'L1_conv_bias2a': _L1_conv_in['bias2a'], 'L1_conv_bias2b': _L1_conv_in['bias2b'], 'L1_conv_bias3a': _L1_conv_in['bias3a'], 'L1_conv_bias3b': _L1_conv_in['bias3b'], 'L1_conv_rscale': _L1_conv_in['rscale'], 'L1_conv_rbias': _L1_conv_in['rbias']}

def reference(x, L0_conv_w1, L0_conv_b1, L0_conv_g1, L0_conv_be1, L0_conv_w2, L0_conv_b2, L0_conv_g2, L0_conv_be2, L0_conv_w3, L0_conv_b3, L0_conv_g3, L0_conv_be3, L0_conv_residual_scale, L1_conv_w1, L1_conv_w2, L1_conv_w3, L1_conv_bias1b, L1_conv_bias2a, L1_conv_bias2b, L1_conv_bias3a, L1_conv_bias3b, L1_conv_rscale, L1_conv_rbias):
    import jax
    import jax.numpy as jnp

    def _L0_conv_ref(x, w1, b1, g1, be1, w2, b2, g2, be2, w3, b3, g3, be3, residual_scale):
        import jax, jax.numpy as jnp
        import numpy as np
        EPS = 1e-05

        def _conv(x, w, b, stride, pad):
            y = jax.lax.conv_general_dilated(x, w, window_strides=(stride, stride), padding=[(pad, pad), (pad, pad)], dimension_numbers=('NCHW', 'OIHW', 'NCHW'))
            return y + b.reshape(1, -1, 1, 1)

        def _bn(x, gamma, beta):
            mean = jnp.mean(x, axis=(0, 2, 3), keepdims=True)
            var = jnp.var(x, axis=(0, 2, 3), keepdims=True)
            xn = (x - mean) * jax.lax.rsqrt(var + EPS)
            return gamma.reshape(1, -1, 1, 1) * xn + beta.reshape(1, -1, 1, 1)
        out = jax.nn.relu(_bn(_conv(x, w1, b1, 1, 0), g1, be1))
        out = jax.nn.relu(_bn(_conv(out, w2, b2, 1, 1), g2, be2))
        out = _bn(_conv(out, w3, b3, 1, 0), g3, be3)
        out = jax.nn.softplus(residual_scale)[0] * out
        out = x + out
        return jax.nn.relu(out)

    def _L1_conv_ref(x, w1, w2, w3, bias1b, bias2a, bias2b, bias3a, bias3b, rscale, rbias):
        import jax, jax.numpy as jnp
        import numpy as np

        def _conv(x, w, padding):
            return jax.lax.conv_general_dilated(x, w, window_strides=(1, 1), padding=padding, dimension_numbers=('NCHW', 'OIHW', 'NCHW'))
        out = _conv(x, w1, 'VALID') + bias1b[0]
        out = _conv(out + bias2a[0], w2, 'SAME') + bias2b[0]
        out = _conv(out + bias3a[0], w3, 'VALID') + bias3b[0]
        return jax.nn.relu(out * rscale[0] + rbias[0] + x)

    def _gn(v, G=32, eps=1e-05):
        B_, C_, H_, W_ = v.shape
        g = v.reshape(B_, G, C_ // G, H_, W_)
        m = jnp.mean(g, axis=(2, 3, 4), keepdims=True)
        s = jnp.var(g, axis=(2, 3, 4), keepdims=True)
        return ((g - m) / jnp.sqrt(s + eps)).reshape(v.shape)

    def _ln_c(v, eps=1e-06):
        m = jnp.mean(v, axis=1, keepdims=True)
        s = jnp.var(v, axis=1, keepdims=True)
        return (v - m) / jnp.sqrt(s + eps)

    def _ln_t(v, eps=1e-05):
        m = jnp.mean(v, axis=-1, keepdims=True)
        s = jnp.var(v, axis=-1, keepdims=True)
        return (v - m) / jnp.sqrt(s + eps)

    def _to_tokens(v):
        B_, C_, H_, W_ = v.shape
        return v.reshape(B_, C_, H_ * W_).transpose(0, 2, 1)

    def _from_tokens(t, like):
        B_, C_, H_, W_ = like.shape
        return t.transpose(0, 2, 1).reshape(B_, C_, H_, W_)
    x = _L0_conv_ref(x, L0_conv_w1, L0_conv_b1, L0_conv_g1, L0_conv_be1, L0_conv_w2, L0_conv_b2, L0_conv_g2, L0_conv_be2, L0_conv_w3, L0_conv_b3, L0_conv_g3, L0_conv_be3, L0_conv_residual_scale)
    x = _L1_conv_ref(x, L1_conv_w1, L1_conv_w2, L1_conv_w3, L1_conv_bias1b, L1_conv_bias2a, L1_conv_bias2b, L1_conv_bias3a, L1_conv_bias3b, L1_conv_rscale, L1_conv_rbias)
    return x

_drawn_inputs = setup_inputs


def setup_inputs(seed=0):
    import zlib

    import numpy as np

    out = dict(_drawn_inputs(seed))
    spreads = {'L0_conv_b1': (0.0, 0.1),
     'L0_conv_g1': (1.0, 0.2),
     'L0_conv_be1': (0.0, 0.1),
     'L0_conv_b2': (0.0, 0.1),
     'L0_conv_g2': (1.0, 0.2),
     'L0_conv_be2': (0.0, 0.1),
     'L0_conv_b3': (0.0, 0.1),
     'L0_conv_g3': (1.0, 0.2),
     'L0_conv_be3': (0.0, 0.1)}
    factors = {}
    for name, (base, spread) in spreads.items():
        noise = np.random.default_rng([zlib.crc32(name.encode()), seed]).standard_normal(out[name].shape)
        drawn = base * np.exp(spread * noise) if base else spread * noise
        out[name] = jnp.asarray(drawn.astype(out[name].dtype))
    for name, factor in factors.items():
        out[name] = (out[name] * factor).astype(out[name].dtype)
    return out
```

```python
from contextlib import ExitStack

import concourse.bass as bass
from concourse import mybir

F32 = mybir.dt.float32
F32R = mybir.dt.float32r
ALU = mybir.AluOpType
ACT = mybir.ActivationFunctionType

P = 128
IMAGES, CHANNELS, H, W = 32, 512, 14, 14
CT = CHANNELS // P
GI = 2
G = IMAGES // GI
N = GI * H * W
PH, PW = H + 2, W + 2
TAPS = 9
W1, W2, W3 = 0, CT, CT + TAPS
WT = CT + TAPS + CT
W12 = CT + TAPS
BANK = 512
BANKS = 8
EPS = 1e-5
TINY = 1e-30
XQ = 4
XS = 4

B1, G1, BE1, B2, G2, BE2, B3, G3, BE3, NPAR = 0, 1, 2, 3, 4, 5, 6, 10, 14, 18
RES_SCALE, RSCALE, RBIAS, BIAS1B, BIAS2A, BIAS2B, BIAS3A, BIAS3B, NSC = 0, 1, 2, 3, 4, 5, 6, 7, 8


def need(engine, sem, value):
    if isinstance(value, int) and value <= 0:
        return
    engine.wait_ge(sem, value)


def build(nc, x_in, w0_in, w1_in, par_in, scal_in, out):
    with ExitStack() as ctx:
        at = -(-nc.sbuf_base // 32) * 32

        def region(size):
            nonlocal at
            start = at
            at += size
            return start

        x_at = region(4 * G * CT * N)
        y_at = region(4 * 2 * G * N)
        a_at = region(4 * G * N)
        stage_at = region(4 * W12 * P)
        wh_at = region(4 * WT * P)
        wl_at = region(4 * WT * P)
        w3_at = region(4 * CT * P)
        pad_at = region(4 * 4 * GI * PH * PW)
        small_at = region(2600)

        def place(name, shape, dtype, offset):
            return nc.alloc_sbuf_tensor_at(name, shape, dtype, offset=offset)

        x = place("x", [P, G, CT, N], F32, x_at)
        y3 = place("y3", [P, 2, G, N], F32, y_at)
        a2 = place("a2", [P, G, N], F32, a_at)
        XB = 4 * CT * N
        xs0 = [(place(f"xh0_{s}", [P, CT, N], F32R, y_at + 4 * G * N + 2 * s * XB),
                place(f"xl0_{s}", [P, CT, N], F32R, y_at + 4 * G * N + (2 * s + 1) * XB)) for s in range(XS)]
        xs1 = [(place(f"xh1_{s}", [P, CT, N], F32R, a_at + 2 * s * XB),
                place(f"xl1_{s}", [P, CT, N], F32R, a_at + (2 * s + 1) * XB)) for s in range(2)]
        stage = place("stage", [P, W12, P], F32, stage_at)
        t2 = [(place(f"t2h_{s}", [P, N], F32R, stage_at + 8 * s * N),
               place(f"t2l_{s}", [P, N], F32R, stage_at + 8 * s * N + 4 * N)) for s in range(2)]
        wh = place("wh", [P, WT, P], F32R, wh_at)
        wl = place("wl", [P, WT, P], F32R, wl_at)
        w3s = place("w3s", [P, CT, P], F32, w3_at)
        PB = 4 * GI * PH * PW
        pads = [(place(f"padh_{s}", [P, PH * GI, PW], F32R, pad_at + 2 * s * PB),
                 place(f"padl_{s}", [P, PH * GI, PW], F32R, pad_at + (2 * s + 1) * PB)) for s in range(2)]

        def small(name, *shape):
            nonlocal small_at
            n = 1
            for d in shape:
                n *= d
            t = place(name, [P, *shape], F32, small_at)
            small_at += 32 * -(-4 * n // 32)
            return t

        par = small("par", NPAR)
        scal = small("scal", NSC)
        stats = small("stats", 2, G, 6)
        mv = small("mv", 2, 2)
        scale1, shift1 = small("scale1", 1), small("shift1", 1)
        scale2, shift2 = small("scale2", 1), small("shift2", 1)
        scale3, shift3 = small("scale3", CT), small("shift3", CT)
        g3s, be3s = small("g3s", CT), small("be3s", CT)
        var_eps, std, r0, q, gr, mb, bd = (small(n, 2) for n in ("var_eps", "std", "r0", "q", "gr", "mb", "bd"))
        sp = small("sp", 8)
        bias_t1, bias_t2, bias_y = small("bias_t1", 1), small("bias_t2", 1), small("bias_y", 1)
        assert small_at <= pad_at + 4 * PB + 2600 and small_at <= nc.sbuf_usable_end

        ps = ctx.enter_context(nc.psum_tensor("ps", [P, BANKS, BANK], F32))

        def sem(name):
            return ctx.enter_context(nc.semaphore(name))

        x_loaded = [sem(f"x_loaded{i}") for i in range(XQ)]
        par_loaded, w0_loaded, w0b_loaded, w1_loaded, w1c_loaded = (
            sem(n) for n in ("par_loaded", "w0_loaded", "w0b_loaded", "w1_loaded", "w1c_loaded"))
        out_stored = sem("out_stored")
        dve_done = sem("dve_done")
        pool_done = sem("pool_done")
        sp_ready, sp_exp, sp_log = sem("sp_ready"), sem("sp_exp"), sem("sp_log")
        w1h_ready, w1l_ready, w2_ready, wb1_ready, wb1c_ready = (
            sem(n) for n in ("w1h_ready", "w1l_ready", "w2_ready", "wb1_ready", "wb1c_ready"))
        pads_zero = sem("pads_zero")
        xh_ready, xl_ready, conv1_done, y1_ready = (sem(n) for n in ("xh_ready", "xl_ready", "conv1_done", "y1_ready"))
        a1_ready, padl_ready, conv2_done, y2_ready = (sem(n) for n in ("a1_ready", "padl_ready", "conv2_done", "y2_ready"))
        stats_done = sem("stats_done")
        var_ready, std_ready, bn_ready = sem("var_ready"), sem("std_ready"), sem("bn_ready")
        a2_ready, conv3_done, y3_ready, applied = (sem(n) for n in ("a2_ready", "conv3_done", "y3_ready", "applied"))
        x1_ready, x1h_ready, x1l_ready, bconv1_done = (sem(n) for n in ("x1_ready", "x1h_ready", "x1l_ready", "bconv1_done"))
        t1h_ready, t1l_ready, bconv2_done = sem("t1h_ready"), sem("t1l_ready"), sem("bconv2_done")
        x1_part, padh_ready = sem("x1_part"), sem("padh_ready")
        t2h_ready, t2l_ready, bconv3_done = sem("t2h_ready"), sem("t2l_ready"), sem("bconv3_done")
        sum_ready, y_ready = sem("sum_ready"), sem("y_ready")

        block = ctx.enter_context(nc.Block())

        def inner(pad):
            return pad[:, GI:GI + GI * H, 1:1 + W]

        def pixels(ap):
            return ap.rearrange("p (r w) -> p r w", w=W)

        def xg(g):
            return x[:, bass.ds(g, 1), :, :].rearrange("p a c n -> p (a c) n")

        def xt(g, c):
            return x[:, bass.ds(g, 1), c, :].rearrange("p a n -> p (a n)")

        def a2g(g):
            return a2[:, bass.ds(g, 1), :].rearrange("p a n -> p (a n)")

        def y3g(half, g):
            return y3[:, half, bass.ds(g, 1), :].rearrange("p a n -> p (a n)")

        @block.sync
        def _(sync):
            def load_x(g, s):
                sync.dma_start(xg(g), x_in[:, bass.ds(g, 1), :, :].rearrange("p a c n -> p (a c) n")).then_inc(x_loaded[s], 16)

            sync.dma_start(stage[:, 0:CT], w0_in[:, 0:CT]).then_inc(w0_loaded, 16)
            for g in range(XQ):
                load_x(g, g)
            sync.dma_start(stage[:, CT:W12], w0_in[:, CT:W12]).then_inc(w0b_loaded, 16)
            sync.dma_start(w3s[:, :, :], w0_in[:, W3:WT]).then_inc(w0b_loaded, 16)
            with sync.Fori(1, G // XQ) as r:
                for s in range(XQ):
                    sync.wait_ge(x_loaded[s], r * 16)
                    load_x(r * XQ + s, s)
            sync.wait_ge(w1l_ready, 1)
            sync.wait_ge(w2_ready, 1)
            sync.dma_start(stage[:, :, :], w1_in[:, 0:W12]).then_inc(w1_loaded, 16)
            sync.wait_ge(conv3_done, 2 * G)
            sync.dma_start(w3s[:, :, :], w1_in[:, W3:WT]).then_inc(w1c_loaded, 16)
            with sync.Fori(0, G) as g:
                sync.wait_ge(y_ready, g + 1)
                sync.dma_start(out[:, bass.ds(g, 1), :, :].rearrange("p a c n -> p (a c) n"), xg(g)).then_inc(out_stored, 16)
            sync.wait_ge(out_stored, 16 * G)

        @block.gpsimd
        def _(pool):
            for padh, padl in pads:
                nc.gpsimd.memset(padh[:, :, :].bitcast(F32), 0.0)
                last = nc.gpsimd.memset(padl[:, :, :].bitcast(F32), 0.0)
            last.then_inc(pads_zero, 1)
            pool.wait_ge(w0b_loaded, 32)
            nc.gpsimd.tensor_copy(wh[:, W2:W12], stage[:, W2:W12]).then_inc(pool_done, 1)
            pool.wait_ge(pool_done, 1)
            nc.gpsimd.tensor_tensor(wl[:, W2:W12], stage[:, W2:W12], wh[:, W2:W12].bitcast(F32), ALU.subtract).then_inc(w2_ready, 1)
            pool.wait_ge(w1_loaded, 16)
            pool.wait_ge(conv2_done, G)
            nc.gpsimd.tensor_copy(wh[:, 0:W12], stage[:, :, :]).then_inc(pool_done, 1)
            pool.wait_ge(pool_done, 2)
            nc.gpsimd.tensor_tensor(wl[:, 0:W12], stage[:, :, :], wh[:, 0:W12].bitcast(F32), ALU.subtract).then_inc(wb1_ready, 1)
            pool.wait_ge(w1c_loaded, 16)
            nc.gpsimd.tensor_copy(wh[:, W3:WT], w3s[:, :, :]).then_inc(pool_done, 1)
            pool.wait_ge(pool_done, 3)
            nc.gpsimd.tensor_tensor(wl[:, W3:WT], w3s[:, :, :], wh[:, W3:WT].bitcast(F32), ALU.subtract).then_inc(wb1c_ready, 1)

        @block.scalar
        def _(act):
            act.dma_start(par[:, :], par_in).then_inc(par_loaded, 16)
            act.dma_start(scal[:, :], scal_in.rearrange("(a n) -> a n", a=1).to_broadcast([P, NSC])).then_inc(par_loaded, 16)
            act.wait_ge(sp_ready, 1)
            nc.scalar.activation(sp[:, 1:2], sp[:, 0:1], ACT.Exp, scale=-1.0).then_inc(sp_exp, 1)
            act.wait_ge(sp_ready, 2)
            nc.scalar.activation(sp[:, 3:4], sp[:, 2:3], ACT.Ln).then_inc(sp_log, 1)
            act.wait_ge(w0_loaded, 16)
            nc.scalar.activation(wh[:, 0:CT], stage[:, 0:CT], ACT.Copy).then_inc(w1h_ready, 1)

            def split_high(g, s, r):
                act.wait_ge(x_loaded[s], 16 * (r + 1))
                need(act, conv1_done, g - XS + 1)
                nc.scalar.activation(xs0[s][0][:, :, :], xg(g), ACT.Copy).then_inc(xh_ready, 1)

            def evacuate1(g, s):
                act.wait_ge(conv1_done, g + 1)
                nc.scalar.activation(y3g(0, g), ps[:, s, 0:N], ACT.Copy).then_inc(y1_ready, 1)

            split_high(0, 0, 0)
            split_high(1, 1, 0)
            for g in range(XS - 2):
                split_high(g + 2, g + 2, 0)
                evacuate1(g, g)
            with act.Fori(1, G // XS) as r:
                for s in range(XS):
                    split_high(r * XS + s, s, r)
                    evacuate1(r * XS + s - 2, (s - 2) % XS)
            for g in range(G - 2, G):
                evacuate1(g, g % XS)

            def square_root(n, w):
                act.wait_ge(var_ready, n)
                nc.scalar.activation(std[:, 0:w], var_eps[:, 0:w], ACT.Sqrt).then_inc(std_ready, 1)
                act.wait_ge(bn_ready, n)

            square_root(1, 1)

            def normalise1(g):
                nc.scalar.activation(y3g(0, g), y3g(0, g), ACT.Relu, bias=shift1[:, 0:1], scale=scale1[:, 0:1]).then_inc(a1_ready, 1)

            def evacuate2(g, s):
                act.wait_ge(conv2_done, g + 1)
                nc.scalar.activation(a2g(g), ps[:, s, 0:N], ACT.Copy).then_inc(y2_ready, 1)

            normalise1(0)
            normalise1(1)
            evacuate2(0, 0)
            with act.Fori(1, G // 2) as r:
                for s in range(2):
                    normalise1(r * 2 + s)
                    evacuate2(r * 2 + s - 1, (s - 1) % 2)
            evacuate2(G - 1, (G - 1) % 2)
            square_root(2, 1)

            def normalise2(r):
                a2r = a2[:, bass.ds(r * 2, 2), :]
                nc.scalar.activation(a2r, a2r, ACT.Relu, bias=shift2[:, 0:1], scale=scale2[:, 0:1]).then_inc(a2_ready, 1)

            def evacuate3(g, s, half, base):
                act.wait_ge(conv3_done, base + g + 1)
                nc.scalar.activation(y3[:, :, bass.ds(g, 1), :].rearrange("p t a n -> p t (a n)"),
                                     ps[:, 2 * s:2 * s + 2, 0:N], ACT.Copy).then_inc(y3_ready, 1)

            normalise2(0)
            with act.Fori(1, G // 2) as r:
                normalise2(r)
                for s in range(2):
                    evacuate3(r * 2 - 2 + s, s, 0, 0)
            for s in range(2):
                evacuate3(G - 2 + s, s, 0, 0)
            square_root(3, 2)
            with act.Fori(0, G // 2) as r:
                for s in range(2):
                    act.wait_ge(applied, r * 2 + s + 1)
                    evacuate3(r * 2 + s, s, 1, G)
            square_root(4, 2)

            def split_high1(g, s):
                act.wait_ge(x1_ready, g + 1)
                need(act, bconv1_done, g - 1)
                nc.scalar.activation(xs1[s][0][:, :, :], xg(g), ACT.Copy).then_inc(x1h_ready, 1)

            def t1_high(g, s):
                act.wait_ge(bconv1_done, g + 1)
                need(act, bconv2_done, g - 1)
                nc.scalar.activation(inner(pads[s][0]), pixels(ps[:, s, 0:N]), ACT.Identity, bias=bias_t1[:, 0:1]).then_inc(t1h_ready, 1)

            def t2_high(g, s):
                act.wait_ge(bconv2_done, g + 1)
                need(act, bconv3_done, g - 1)
                nc.scalar.activation(t2[s][0][:, :], ps[:, 2 + s, 0:N], ACT.Identity, bias=bias_t2[:, 0:1]).then_inc(t2h_ready, 1)

            def finish(g):
                act.wait_ge(sum_ready, g + 1)
                nc.scalar.activation(xg(g), xg(g), ACT.Relu, bias=bias_y[:, 0:1]).then_inc(y_ready, 1)

            split_high1(0, 0)
            split_high1(1, 1)
            t1_high(0, 0)
            split_high1(2, 0)
            t1_high(1, 1)
            t2_high(0, 0)
            t1_high(2, 0)
            split_high1(3, 1)
            t2_high(1, 1)
            with act.Fori(0, (G - 4) // 2) as r:
                for s in range(2):
                    g = r * 2 + s + 1
                    t1_high(g + 2, (s + 1) % 2)
                    finish(g - 1)
                    split_high1(g + 3, s % 2)
                    t2_high(g + 1, s % 2)
            t1_high(G - 1, (G - 1) % 2)
            finish(G - 4)
            t2_high(G - 2, (G - 2) % 2)
            finish(G - 3)
            t2_high(G - 1, (G - 1) % 2)
            finish(G - 2)
            finish(G - 1)

        @block.vector
        def _(dve):
            steps = [0]

            def chain(instruction):
                steps[0] += 1
                instruction.then_inc(dve_done, 1)
                dve.wait_ge(dve_done, steps[0])

            dve.wait_ge(par_loaded, 32)
            s_ = scal[:, RES_SCALE:RES_SCALE + 1]
            nc.vector.scalar_tensor_tensor(sp[:, 0:1], s_, -1.0, s_, ALU.mult, ALU.max).then_inc(sp_ready, 1)
            dve.wait_ge(sp_exp, 1)
            nc.vector.tensor_scalar(sp[:, 2:3], sp[:, 1:2], 1.0, None, ALU.add).then_inc(sp_ready, 1)
            dve.wait_ge(sp_ready, 2)
            chain(nc.vector.tensor_scalar(sp[:, 4:5], sp[:, 2:3], -1.0, TINY, ALU.add, ALU.add))
            chain(nc.vector.reciprocal(sp[:, 5:6], sp[:, 4:5]))
            dve.wait_ge(sp_log, 1)
            chain(nc.vector.scalar_tensor_tensor(sp[:, 6:7], sp[:, 3:4], TINY, sp[:, 5:6], ALU.add, ALU.mult))
            chain(nc.vector.tensor_tensor(sp[:, 4:5], sp[:, 6:7], sp[:, 1:2], ALU.mult))
            chain(nc.vector.scalar_tensor_tensor(sp[:, 7:8], s_, 0.0, sp[:, 4:5], ALU.max, ALU.add))
            nc.vector.tensor_scalar(g3s[:, :], par[:, G3:G3 + CT], sp[:, 7:8], None, ALU.mult)
            nc.vector.tensor_scalar(be3s[:, :], par[:, BE3:BE3 + CT], sp[:, 7:8], None, ALU.mult)

            def sc(c):
                return scal[:, c:c + 1]
            nc.vector.tensor_tensor(bias_t1[:, :], sc(BIAS1B), sc(BIAS2A), ALU.add)
            nc.vector.tensor_tensor(bias_t2[:, :], sc(BIAS2B), sc(BIAS3A), ALU.add)
            chain(nc.vector.scalar_tensor_tensor(bias_y[:, :], sc(BIAS3B), sc(RSCALE), sc(RBIAS), ALU.mult, ALU.add))

            dve.wait_ge(w1h_ready, 1)
            nc.vector.tensor_tensor(wl[:, 0:CT], stage[:, 0:CT], wh[:, 0:CT].bitcast(F32), ALU.subtract).then_inc(w1l_ready, 1)

            def split_low(g, s):
                dve.wait_ge(xh_ready, g + 1)
                nc.vector.tensor_tensor(xs0[s][1][:, :, :], xg(g), xs0[s][0][:, :, :].bitcast(F32), ALU.subtract).then_inc(xl_ready, 1)

            def gather(half, g, y, ready, count):
                dve.wait_ge(ready, count)
                nc.vector.bn_stats(stats[:, half, bass.ds(g, 1), :].rearrange("p a n -> p (a n)"), y).then_inc(stats_done, 1)

            split_low(0, 0)
            split_low(1, 1)
            for g in range(XS - 2):
                split_low(g + 2, g + 2)
                gather(0, g, y3g(0, g), y1_ready, g + 1)
            with dve.Fori(1, G // XS) as r:
                for s in range(XS):
                    split_low(r * XS + s, s)
                    gather(0, r * XS + s - 2, y3g(0, r * XS + s - 2), y1_ready, r * XS + s - 1)
            for g in range(G - 2, G):
                gather(0, g, y3g(0, g), y1_ready, g + 1)

            def batch_norm(n, w, stats_count, bias, gamma, beta, scale, shift):
                dve.wait_ge(stats_done, stats_count)
                for half in range(w):
                    last = nc.vector.bn_aggr(mv[:, half, :], stats[:, half].rearrange("p g s -> p (g s)"))
                chain(last)
                mean, var = mv[:, 0:w, 0], mv[:, 0:w, 1]
                nc.vector.tensor_scalar(var_eps[:, 0:w], var, EPS, None, ALU.add).then_inc(var_ready, 1)
                chain(nc.vector.tensor_tensor(mb[:, 0:w], mean, bias, ALU.add))
                chain(nc.vector.tensor_tensor(bd[:, 0:w], bias, mb[:, 0:w], ALU.subtract))
                dve.wait_ge(std_ready, n)
                chain(nc.vector.reciprocal(r0[:, 0:w], std[:, 0:w]))
                nc.vector.tensor_tensor(gr[:, 0:w], r0[:, 0:w], gamma, ALU.mult)
                chain(nc.vector.tensor_tensor(q[:, 0:w], r0[:, 0:w], r0[:, 0:w], ALU.mult))
                chain(nc.vector.tensor_tensor(q[:, 0:w], q[:, 0:w], var_eps[:, 0:w], ALU.mult))
                chain(nc.vector.tensor_scalar(q[:, 0:w], q[:, 0:w], -0.5, 1.5, ALU.mult, ALU.add))
                chain(nc.vector.tensor_tensor(scale, gr[:, 0:w], q[:, 0:w], ALU.mult))
                chain(nc.vector.tensor_tensor(bd[:, 0:w], bd[:, 0:w], scale, ALU.mult))
                steps[0] += 1
                nc.vector.tensor_tensor(shift, bd[:, 0:w], beta, ALU.add).then_inc(bn_ready, 1)
                dve.wait_ge(bn_ready, n)
                steps[0] -= 1

            def col(c, w=1):
                return par[:, c:c + w]

            batch_norm(1, 1, G, col(B1), col(G1), col(BE1), scale1[:, :], shift1[:, :])

            def split1(g, s):
                need(dve, conv2_done, g - 1)
                dve.wait_ge(a1_ready, g + 1)
                nc.vector.tensor_scalar(inner(pads[s][0]), pixels(y3g(0, g)), 1.0, None, ALU.mult).then_inc(padh_ready, 1)
                dve.wait_ge(padh_ready, g + 1)
                nc.vector.tensor_tensor(inner(pads[s][1]), pixels(y3g(0, g)), inner(pads[s][0]).bitcast(F32), ALU.subtract).then_inc(padl_ready, 1)

            dve.wait_ge(pads_zero, 1)
            split1(0, 0)
            split1(1, 1)
            gather(0, 0, a2g(0), y2_ready, 1)
            with dve.Fori(1, G // 2) as r:
                for s in range(2):
                    split1(r * 2 + s, s)
                    gather(0, r * 2 + s - 1, a2g(r * 2 + s - 1), y2_ready, r * 2 + s)
            gather(0, G - 1, a2g(G - 1), y2_ready, G)
            batch_norm(2, 1, 2 * G, col(B2), col(G2), col(BE2), scale2[:, :], shift2[:, :])

            with dve.Fori(0, G) as g:
                dve.wait_ge(y3_ready, g + 1)
                for half in range(2):
                    nc.vector.bn_stats(stats[:, half, bass.ds(g, 1), :].rearrange("p a n -> p (a n)"), y3g(half, g)).then_inc(stats_done, 1)
            batch_norm(3, 2, 4 * G, col(B3, 2), g3s[:, 0:2], be3s[:, 0:2], scale3[:, 0:2], shift3[:, 0:2])

            def apply(g, half, c):
                return nc.vector.scalar_tensor_tensor(xt(g, c), y3g(half, g), scale3[:, c:c + 1], xt(g, c), ALU.mult, ALU.add)

            def stats23(g):
                dve.wait_ge(y3_ready, g + (G + 1))
                for half in range(2):
                    nc.vector.bn_stats(stats[:, half, bass.ds(g, 1), :].rearrange("p a n -> p (a n)"), y3g(half, g)).then_inc(stats_done, 1)

            apply(0, 0, 0)
            apply(0, 1, 1).then_inc(applied, 1)
            with dve.Fori(1, G) as g:
                apply(g, 0, 0)
                apply(g, 1, 1).then_inc(applied, 1)
                stats23(g - 1)
            stats23(G - 1)
            batch_norm(4, 2, 6 * G, col(B3 + 2, 2), g3s[:, 2:4], be3s[:, 2:4], scale3[:, 2:4], shift3[:, 2:4])

            def block0_result(g):
                apply(g, 0, 2)
                apply(g, 1, 3).then_inc(x1_part, 1)
                for c in range(2):
                    nc.vector.tensor_scalar(xt(g, c), xt(g, c), shift3[:, c:c + 1], 0.0, ALU.add, ALU.max)
                dve.wait_ge(x1_part, g + 1)
                for c in range(2, 4):
                    last = nc.vector.tensor_scalar(xt(g, c), xt(g, c), shift3[:, c:c + 1], 0.0, ALU.add, ALU.max)
                last.then_inc(x1_ready, 1)

            def split_low1(g, s):
                dve.wait_ge(x1h_ready, g + 1)
                nc.vector.tensor_tensor(xs1[s][1][:, :, :], xg(g), xs1[s][0][:, :, :].bitcast(F32), ALU.subtract).then_inc(x1l_ready, 1)

            def t1_low(g, s):
                dve.wait_ge(t1h_ready, g + 1)
                nc.vector.scalar_tensor_tensor(inner(pads[s][1]), pixels(ps[:, s, 0:N]), bias_t1[:, 0:1], inner(pads[s][0]).bitcast(F32),
                                               ALU.add, ALU.subtract).then_inc(t1l_ready, 1)

            def t2_low(g, s):
                dve.wait_ge(t2h_ready, g + 1)
                nc.vector.scalar_tensor_tensor(t2[s][1][:, :], ps[:, 2 + s, 0:N], bias_t2[:, 0:1], t2[s][0][:, :].bitcast(F32),
                                               ALU.add, ALU.subtract).then_inc(t2l_ready, 1)

            def add_result(g):
                dve.wait_ge(bconv3_done, g + 1)
                nc.vector.scalar_tensor_tensor(xg(g), ps[:, 4:8, 0:N], scal[:, RSCALE:RSCALE + 1], xg(g),
                                               ALU.mult, ALU.add).then_inc(sum_ready, 1)

            block0_result(0)
            split_low1(0, 0)
            block0_result(1)
            split_low1(1, 1)
            block0_result(2)
            t1_low(0, 0)
            split_low1(2, 0)
            t1_low(1, 1)
            t2_low(0, 0)
            block0_result(3)
            t1_low(2, 0)
            split_low1(3, 1)
            t2_low(1, 1)
            with dve.Fori(0, (G - 4) // 2) as r:
                for s in range(2):
                    g = r * 2 + s + 1
                    add_result(g - 1)
                    block0_result(g + 3)
                    t1_low(g + 2, (s + 1) % 2)
                    split_low1(g + 3, s % 2)
                    t2_low(g + 1, s % 2)
            add_result(G - 4)
            t1_low(G - 1, (G - 1) % 2)
            t2_low(G - 2, (G - 2) % 2)
            add_result(G - 3)
            t2_low(G - 1, (G - 1) % 2)
            add_result(G - 2)
            add_result(G - 1)

        @block.tensor
        def _(pe):
            def products(bank, terms):
                passes = [p for t, vh, vl in terms for p in ((wh, t, vh), (wh, t, vl), (wl, t, vh))]
                for i, (w, t, v) in enumerate(passes):
                    last = nc.tensor.matmul(ps[:, bank, 0:N], w[:, t, :], v, start=i == 0, stop=i == len(passes) - 1)
                return last

            def taps(pad):
                return [pad[:, k // 3 * GI:(k // 3 + H) * GI, k % 3:k % 3 + W] for k in range(TAPS)]

            def conv_1x1(bank, split):
                return products(bank, [(W1 + c, split[0][:, c, :], split[1][:, c, :]) for c in range(CT)])

            def conv_3x3(bank, pad):
                return products(bank, [(W2 + k, h, l) for k, (h, l) in enumerate(zip(taps(pad[0]), taps(pad[1])))])

            def conv1(g, s):
                pe.wait_ge(xl_ready, g + 1)
                need(pe, y1_ready, g - XS + 1)
                conv_1x1(s, xs0[s]).then_inc(conv1_done, 1)

            pe.wait_ge(w1l_ready, 1)
            for s in range(XS):
                conv1(s, s)
            with pe.Fori(1, G // XS) as r:
                for s in range(XS):
                    conv1(r * XS + s, s)

            def conv2(g, s):
                pe.wait_ge(padl_ready, g + 1)
                need(pe, y2_ready, g - 1)
                conv_3x3(s, pads[s]).then_inc(conv2_done, 1)

            pe.wait_ge(w2_ready, 1)
            for s in range(2):
                conv2(s, s)
            with pe.Fori(1, G // 2) as r:
                for s in range(2):
                    conv2(r * 2 + s, s)

            def conv3(g, s, tile, base):
                need(pe, y3_ready, base + g - 1)
                for t in range(2):
                    last = nc.tensor.matmul(ps[:, 2 * s + t, 0:N], w3s[:, tile + t, :], a2g(g), start=True, stop=True)
                last.then_inc(conv3_done, 1)

            for tile, base in ((0, 0), (2, G)):
                def pair(r):
                    if tile == 0:
                        pe.wait_ge(a2_ready, r + 1)
                    for s in range(2):
                        conv3(r * 2 + s, s, tile, base)
                pair(0)
                with pe.Fori(1, G // 2) as r:
                    pair(r)

            def b_conv1(g, s):
                pe.wait_ge(x1l_ready, g + 1)
                need(pe, t1l_ready, g - 1)
                conv_1x1(s, xs1[s]).then_inc(bconv1_done, 1)

            def b_conv2(g, s):
                pe.wait_ge(t1l_ready, g + 1)
                need(pe, t2l_ready, g - 1)
                conv_3x3(2 + s, pads[s]).then_inc(bconv2_done, 1)

            def b_conv3(g, s):
                pe.wait_ge(t2l_ready, g + 1)
                need(pe, sum_ready, g)
                for c in range(CT):
                    last = products(4 + c, [(W3 + c, t2[s][0][:, :], t2[s][1][:, :])])
                last.then_inc(bconv3_done, 1)

            pe.wait_ge(wb1_ready, 1)
            b_conv1(0, 0)
            b_conv1(1, 1)
            b_conv2(0, 0)
            pe.wait_ge(wb1c_ready, 1)
            for g in range(2):
                b_conv1(g + 2, g)
                b_conv2(g + 1, 1 - g)
                b_conv3(g, g)
            with pe.Fori(1, (G - 2) // 2) as r:
                for s in range(2):
                    g = r * 2 + s
                    b_conv1(g + 2, s)
                    b_conv2(g + 1, 1 - s)
                    b_conv3(g, s)
            b_conv2(G - 1, 1)
            b_conv3(G - 2, 0)
            b_conv3(G - 1, 1)


def kernel(x, L0_conv_w1, L0_conv_b1, L0_conv_g1, L0_conv_be1, L0_conv_w2, L0_conv_b2, L0_conv_g2, L0_conv_be2,
           L0_conv_w3, L0_conv_b3, L0_conv_g3, L0_conv_be3, L0_conv_residual_scale, L1_conv_w1, L1_conv_w2,
           L1_conv_w3, L1_conv_bias1b, L1_conv_bias2a, L1_conv_bias2b, L1_conv_bias3a, L1_conv_bias3b,
           L1_conv_rscale, L1_conv_rbias):
    import numpy as np
    import concourse.bacc as bacc
    from concourse.bass_utils import run_bass_kernel_spmd

    def weights(w1, w2, w3):
        a = np.asarray(w1).reshape(P, CT, P).transpose(2, 1, 0)
        b = np.asarray(w2).reshape(P, P, TAPS).transpose(1, 2, 0)
        c = np.asarray(w3).reshape(CT, P, P).transpose(2, 0, 1)
        return np.ascontiguousarray(np.concatenate([a, b, c], axis=1))

    def columns(*vectors):
        return np.ascontiguousarray(np.concatenate([np.asarray(v).reshape(-1, P).T for v in vectors], axis=1))

    arrays = {
        "x_dram": np.ascontiguousarray(np.asarray(x).reshape(G, GI, CT, P, H, W).transpose(3, 0, 2, 4, 1, 5)).reshape(P, G, CT, N),
        "w0_dram": weights(L0_conv_w1, L0_conv_w2, L0_conv_w3),
        "w1_dram": weights(L1_conv_w1, L1_conv_w2, L1_conv_w3),
        "par_dram": columns(L0_conv_b1, L0_conv_g1, L0_conv_be1, L0_conv_b2, L0_conv_g2, L0_conv_be2,
                            L0_conv_b3, L0_conv_g3, L0_conv_be3),
        "scal_dram": np.concatenate([np.asarray(v) for v in (
            L0_conv_residual_scale, L1_conv_rscale, L1_conv_rbias, L1_conv_bias1b, L1_conv_bias2a,
            L1_conv_bias2b, L1_conv_bias3a, L1_conv_bias3b)]),
    }
    nc = bacc.Bacc("TRN2", target_bir_lowering=False, num_devices=1)
    args = [nc.dram_tensor(n, a.shape, mybir.dt.from_np(a.dtype), kind="ExternalInput").ap() for n, a in arrays.items()]
    out = nc.dram_tensor("out_dram", (P, G, CT, N), F32, kind="ExternalOutput").ap()
    build(nc, *args, out)
    r = run_bass_kernel_spmd(nc, [arrays], core_ids=[0])
    y = r.results[0]["out_dram"].reshape(P, G, CT, H, GI, W).transpose(1, 4, 2, 0, 3, 5)
    return np.ascontiguousarray(y).reshape(IMAGES, CHANNELS, H, W)
```

```python
from contextlib import ExitStack

import concourse.bass as bass
from concourse import mybir

F32 = mybir.dt.float32
F32R = mybir.dt.float32r
ALU = mybir.AluOpType
ACT = mybir.ActivationFunctionType

P = 128
IMAGES, CHANNELS, H, W = 32, 512, 14, 14
CT = CHANNELS // P
GI = 2
G = IMAGES // GI
N = GI * H * W
PH, PW = H + 2, W + 2
TAPS = 9
W1, W2, W3 = 0, CT, CT + TAPS
WT = CT + TAPS + CT
W12 = CT + TAPS
BANK = 512
BANKS = 8
EPS = 1e-5
TINY = 1e-30
XQ = 4
XS = 4

B1, G1, BE1, B2, G2, BE2, B3, G3, BE3, NPAR = 0, 1, 2, 3, 4, 5, 6, 10, 14, 18
RES_SCALE, RSCALE, RBIAS, BIAS1B, BIAS2A, BIAS2B, BIAS3A, BIAS3B, NSC = 0, 1, 2, 3, 4, 5, 6, 7, 8


def need(engine, sem, value):
    if isinstance(value, int) and value <= 0:
        return
    engine.wait_ge(sem, value)


def build(nc, x_in, w0_in, w1_in, par_in, scal_in, out):
    with ExitStack() as ctx:
        at = -(-nc.sbuf_base // 32) * 32

        def region(size):
            nonlocal at
            start = at
            at += size
            return start

        x_at = region(4 * G * CT * N)
        y_at = region(4 * 2 * G * N)
        a_at = region(4 * G * N)
        stage_at = region(4 * W12 * P)
        wh_at = region(4 * WT * P)
        wl_at = region(4 * WT * P)
        w3_at = region(4 * CT * P)
        pad_at = region(4 * 4 * GI * PH * PW)
        small_at = region(2600)

        def place(name, shape, dtype, offset):
            return nc.alloc_sbuf_tensor_at(name, shape, dtype, offset=offset)

        x = place("x", [P, G, CT, N], F32, x_at)
        y3 = place("y3", [P, 2, G, N], F32, y_at)
        a2 = place("a2", [P, G, N], F32, a_at)
        XB = 4 * CT * N
        xs0 = [(place(f"xh0_{s}", [P, CT, N], F32R, y_at + 4 * G * N + 2 * s * XB),
                place(f"xl0_{s}", [P, CT, N], F32R, y_at + 4 * G * N + (2 * s + 1) * XB)) for s in range(XS)]
        xs1 = [(place(f"xh1_{s}", [P, CT, N], F32R, a_at + 2 * s * XB),
                place(f"xl1_{s}", [P, CT, N], F32R, a_at + (2 * s + 1) * XB)) for s in range(2)]
        stage = place("stage", [P, W12, P], F32, stage_at)
        t2 = [(place(f"t2h_{s}", [P, N], F32R, stage_at + 8 * s * N),
               place(f"t2l_{s}", [P, N], F32R, stage_at + 8 * s * N + 4 * N)) for s in range(2)]
        wh = place("wh", [P, WT, P], F32R, wh_at)
        wl = place("wl", [P, WT, P], F32R, wl_at)
        w3s = place("w3s", [P, CT, P], F32, w3_at)
        PB = 4 * GI * PH * PW
        pads = [(place(f"padh_{s}", [P, PH * GI, PW], F32R, pad_at + 2 * s * PB),
                 place(f"padl_{s}", [P, PH * GI, PW], F32R, pad_at + (2 * s + 1) * PB)) for s in range(2)]

        def small(name, *shape):
            nonlocal small_at
            n = 1
            for d in shape:
                n *= d
            t = place(name, [P, *shape], F32, small_at)
            small_at += 32 * -(-4 * n // 32)
            return t

        par = small("par", NPAR)
        scal = small("scal", NSC)
        stats = small("stats", 2, G, 6)
        mv = small("mv", 2)
        scale1, shift1 = small("scale1", 1), small("shift1", 1)
        scale2, shift2 = small("scale2", 1), small("shift2", 1)
        scale3, shift3 = small("scale3", CT), small("shift3", CT)
        g3s, be3s = small("g3s", CT), small("be3s", CT)
        one = small("one", 1)
        warm = place("warm", [P, N], mybir.dt.bfloat16, small_at)
        small_at += 32 * -(-2 * N // 32)
        var_eps, std, r0, vrr, gr, mean_off = (small(n, 1) for n in ("var_eps", "std", "r0", "vrr", "gr", "mean_off"))
        half_g = small("half_g", 2 + CT)
        sp = small("sp", 8)
        bias_t1, bias_t2, bias_y = small("bias_t1", 1), small("bias_t2", 1), small("bias_y", 1)
        assert small_at <= pad_at + 4 * PB + 2600 and small_at <= nc.sbuf_usable_end

        ps = ctx.enter_context(nc.psum_tensor("ps", [P, BANKS, BANK], F32))

        def sem(name):
            return ctx.enter_context(nc.semaphore(name))

        x0_loaded = [sem(f"x0_loaded{c}") for c in range(CT)]
        x0h_ready, x0l_ready = sem("x0h_ready"), sem("x0l_ready")
        w03_loaded = sem("w03_loaded")
        mean_ready, a2_scaled, a2b_ready = sem("mean_ready"), sem("a2_scaled"), sem("a2b_ready")
        one_ready, half_ready, warm_ready = sem("one_ready"), sem("half_ready"), sem("warm_ready")
        xl3_ready, w2h_ready = sem("xl3_ready"), sem("w2h_ready")
        x15h_ready, x15l_ready = sem("x15h_ready"), sem("x15l_ready")
        scaled0, scaled1, x1_first, first_h, first_l = (
            sem(n) for n in ("scaled0", "scaled1", "x1_first", "first_h", "first_l"))
        x1_relu, last_h, last_l, tile2_applied = (sem(n) for n in ("x1_relu", "last_h", "last_l", "tile2_applied"))
        last_sum = sem("last_sum")
        x_loaded = [sem(f"x_loaded{i}") for i in range(XQ)]
        par_loaded, w0_loaded, w0b_loaded, w1_loaded, w1c_loaded = (
            sem(n) for n in ("par_loaded", "w0_loaded", "w0b_loaded", "w1_loaded", "w1c_loaded"))
        out_stored = sem("out_stored")
        dve_done = sem("dve_done")
        pool_done = sem("pool_done")
        sp_ready, sp_exp, sp_log = sem("sp_ready"), sem("sp_exp"), sem("sp_log")
        w1h_ready, w1l_ready, w2_ready, wb1_ready, wb1c_ready = (
            sem(n) for n in ("w1h_ready", "w1l_ready", "w2_ready", "wb1_ready", "wb1c_ready"))
        pads_zero = sem("pads_zero")
        xh_ready, xl_ready, conv1_done, y1_ready = (sem(n) for n in ("xh_ready", "xl_ready", "conv1_done", "y1_ready"))
        a1_ready, padl_ready, conv2_done, y2_ready = (sem(n) for n in ("a1_ready", "padl_ready", "conv2_done", "y2_ready"))
        stats_done = sem("stats_done")
        var_ready, std_ready, bn_ready = sem("var_ready"), sem("std_ready"), sem("bn_ready")
        a2_ready, conv3_done, y3_ready, applied0, added0, added1 = (
            sem(n) for n in ("a2_ready", "conv3_done", "y3_ready", "applied0", "added0", "added1"))
        x1_ready, x1h_ready, x1l_ready, bconv1_done = (sem(n) for n in ("x1_ready", "x1h_ready", "x1l_ready", "bconv1_done"))
        t1h_ready, t1l_ready, bconv2_done = sem("t1h_ready"), sem("t1l_ready"), sem("bconv2_done")
        x1_part, padh_ready = sem("x1_part"), sem("padh_ready")
        t2h_ready, t2l_ready, bconv3_done = sem("t2h_ready"), sem("t2l_ready"), sem("bconv3_done")
        sum_ready, y_ready = sem("sum_ready"), sem("y_ready")

        block = ctx.enter_context(nc.Block())

        def inner(pad):
            return pad[:, GI:GI + GI * H, 1:1 + W]

        def pixels(ap):
            return ap.rearrange("p (r w) -> p r w", w=W)

        def xg(g):
            return x[:, bass.ds(g, 1), :, :].rearrange("p a c n -> p (a c) n")

        def xt(g, c):
            return x[:, bass.ds(g, 1), c, :].rearrange("p a n -> p (a n)")

        def a2g(g):
            return a2[:, bass.ds(g, 1), :].rearrange("p a n -> p (a n)")

        def y3g(half, g):
            return y3[:, half, bass.ds(g, 1), :].rearrange("p a n -> p (a n)")

        def y3p(half, r):
            return y3[:, half, bass.ds(r * 2, 2), :]

        def xp(r, c):
            return x[:, bass.ds(r * 2, 2), c, :]

        R = G // 2
        SLOTS = BANKS // 2

        @block.sync
        def _(sync):
            def load_x(g, s):
                sync.dma_start(xg(g), x_in[:, bass.ds(g, 1), :, :].rearrange("p a c n -> p (a c) n")).then_inc(x_loaded[s], 16)

            sync.dma_start(stage[:, 0:CT], w0_in[:, 0:CT]).then_inc(w0_loaded, 16)
            for c in range(CT):
                sync.dma_start(x[:, 0, c, :], x_in[:, 0, c, :]).then_inc(x0_loaded[c], 16)
            for g in range(1, XQ):
                load_x(g, g)
            for c in range(CT):
                sync.wait_ge(x0_loaded[c], 16)
            load_x(XQ, 0)
            with sync.Fori(1, G // XQ - 1) as r:
                for s in range(1, XQ + 1):
                    sync.wait_ge(x_loaded[s % XQ], r * 16)
                    load_x(r * XQ + s, s % XQ)
            for s in range(1, XQ):
                sync.wait_ge(x_loaded[s], (G // XQ - 1) * 16)
                load_x(G - XQ + s, s)
            sync.dma_start(stage[:, CT:W12], w0_in[:, CT:W12]).then_inc(w0b_loaded, 16)
            sync.dma_start(w3s[:, :, :], w0_in[:, W3:WT]).then_inc(w03_loaded, 16)
            sync.wait_ge(w1l_ready, 1)
            sync.wait_ge(w2_ready, 1)
            sync.dma_start(stage[:, :, :], w1_in[:, 0:W12]).then_inc(w1_loaded, 16)
            sync.wait_ge(conv3_done, CT * R)
            sync.dma_start(w3s[:, :, :], w1_in[:, W3:WT]).then_inc(w1c_loaded, 16)
            with sync.Fori(0, G - 1) as g:
                sync.wait_ge(y_ready, g + 1)
                sync.dma_start(out[:, bass.ds(g, 1), :, :].rearrange("p a c n -> p (a c) n"), xg(g)).then_inc(out_stored, 16)
            for c in range(CT):
                sync.wait_ge(y_ready, G + c)
                sync.dma_start(out[:, G - 1, c, :], x[:, G - 1, c, :]).then_inc(out_stored, 16)
            sync.wait_ge(out_stored, 16 * (G - 1 + CT))

        @block.gpsimd
        def _(pool):
            for padh, padl in pads:
                nc.gpsimd.memset(padh[:, :, :].bitcast(F32), 0.0)
                last = nc.gpsimd.memset(padl[:, :, :].bitcast(F32), 0.0)
            last.then_inc(pads_zero, 1)
            def split_low3(g, s):
                pool.wait_ge(xh_ready, g)
                nc.gpsimd.tensor_tensor(xs0[s][1][:, CT - 1, :], xt(g, CT - 1), xs0[s][0][:, CT - 1, :].bitcast(F32), ALU.subtract).then_inc(xl3_ready, 1)

            for s in range(1, XS):
                split_low3(s, s)
            with pool.Fori(1, G // XS - 1) as r:
                for s in range(XS):
                    split_low3(r * XS + s, s)
            for s in range(XS - 1):
                split_low3(G - XS + s, s)
            pool.wait_ge(w2h_ready, 1)
            nc.gpsimd.tensor_tensor(wl[:, W2:W12], stage[:, W2:W12], wh[:, W2:W12].bitcast(F32), ALU.subtract).then_inc(w2_ready, 1)
            pool.wait_ge(w1_loaded, 16)
            pool.wait_ge(conv2_done, G)
            nc.gpsimd.tensor_copy(wh[:, 0:W12], stage[:, :, :]).then_inc(pool_done, 1)
            pool.wait_ge(pool_done, 1)
            nc.gpsimd.tensor_tensor(wl[:, 0:W12], stage[:, :, :], wh[:, 0:W12].bitcast(F32), ALU.subtract).then_inc(wb1_ready, 1)
            with pool.Fori(0, R // 2) as k:
                pool.wait_ge(scaled0, k + 1)
                nc.gpsimd.tensor_tensor(xp(k * 2, 0), xp(k * 2, 0), y3p(0, k * 2), ALU.add).then_inc(added0, 1)
            with pool.Fori(0, R) as r:
                pool.wait_ge(scaled1, r + 1)
                nc.gpsimd.tensor_tensor(xp(r, 1), xp(r, 1), y3p(1, r), ALU.add).then_inc(added1, 1)
            for c in range(3):
                pool.wait_ge(first_h, c + 1)
                nc.gpsimd.tensor_tensor(xs1[0][1][:, c, :], x[:, 0, c, :], xs1[0][0][:, c, :].bitcast(F32), ALU.subtract).then_inc(first_l, 1)
            pool.wait_ge(w1c_loaded, 16)
            nc.gpsimd.tensor_copy(wh[:, W3:WT], w3s[:, :, :]).then_inc(pool_done, 1)
            pool.wait_ge(pool_done, 2)
            nc.gpsimd.tensor_tensor(wl[:, W3:WT], w3s[:, :, :], wh[:, W3:WT].bitcast(F32), ALU.subtract).then_inc(wb1c_ready, 1)

        @block.scalar
        def _(act):
            act.dma_start(par[:, :], par_in).then_inc(par_loaded, 16)
            act.dma_start(scal[:, :], scal_in.rearrange("(a n) -> a n", a=1).to_broadcast([P, NSC])).then_inc(par_loaded, 16)
            act.wait_ge(one_ready, 1)
            nc.scalar.activation(std[:, 0:1], one[:, 0:1], ACT.Sqrt)
            act.wait_ge(w0_loaded, 16)
            nc.scalar.activation(wh[:, 0:CT], stage[:, 0:CT], ACT.Copy).then_inc(w1h_ready, 1)

            def split_high(g, s, r):
                act.wait_ge(x_loaded[s], 16 * (r + (0 if s == 0 else 1)))
                need(act, conv1_done, g - XS + 1)
                nc.scalar.activation(xs0[s][0][:, :, :], xg(g), ACT.Copy).then_inc(xh_ready, 1)

            def evacuate1(g, s):
                act.wait_ge(conv1_done, g + 1)
                nc.scalar.activation(y3g(0, g), ps[:, s, 0:N], ACT.Copy).then_inc(y1_ready, 1)

            for c in range(CT):
                act.wait_ge(x0_loaded[c], 16)
                nc.scalar.activation(xs0[0][0][:, c, :], x[:, 0, c, :], ACT.Copy).then_inc(x0h_ready, 1)
            split_high(1, 1, 0)
            for g in range(XS - 2):
                split_high(g + 2, g + 2, 0)
                evacuate1(g, g)
            with act.Fori(1, G // XS - 1) as r:
                for s in range(XS):
                    split_high(r * XS + s, s, r)
                    evacuate1(r * XS + s - 2, (s - 2) % XS)
            for s in range(XS - 1):
                split_high(G - XS + s, s, G // XS - 1)
                evacuate1(G - XS + s - 2, (s - 2) % XS)
            act.wait_ge(x_loaded[XS - 1], 16 * (G // XS))
            act.wait_ge(conv1_done, G - XS)
            for c in range(CT):
                nc.scalar.activation(xs0[XS - 1][0][:, c, :], x[:, G - 1, c, :], ACT.Copy).then_inc(x15h_ready, 1)
            for g in range(G - 3, G):
                evacuate1(g, g % XS)
            act.wait_ge(w0b_loaded, 16)
            nc.scalar.activation(wh[:, W2:W12], stage[:, W2:W12], ACT.Copy).then_inc(w2h_ready, 1)

            def square_root(n):
                act.wait_ge(var_ready, n)
                nc.scalar.activation(std[:, :], var_eps[:, :], ACT.Sqrt).then_inc(std_ready, 1)

            square_root(1)
            act.wait_ge(bn_ready, 1)

            def normalise1(g):
                nc.scalar.activation(y3g(0, g), y3g(0, g), ACT.Relu, bias=shift1[:, 0:1], scale=scale1[:, 0:1]).then_inc(a1_ready, 1)

            def evacuate2(g, s):
                act.wait_ge(conv2_done, g + 1)
                nc.scalar.activation(a2g(g), ps[:, s, 0:N], ACT.Copy).then_inc(y2_ready, 1)

            normalise1(0)
            normalise1(1)
            act.wait_ge(sp_ready, 1)
            nc.scalar.activation(sp[:, 1:2], sp[:, 0:1], ACT.Exp, scale=-1.0).then_inc(sp_exp, 1)
            act.wait_ge(sp_ready, 2)
            nc.scalar.activation(sp[:, 3:4], sp[:, 2:3], ACT.Ln).then_inc(sp_log, 1)
            nc.scalar.activation(std[:, 0:1], one[:, 0:1], ACT.Sqrt)
            evacuate2(0, 0)
            with act.Fori(1, G // 2) as r:
                for s in range(2):
                    normalise1(r * 2 + s)
                    evacuate2(r * 2 + s - 1, (s - 1) % 2)
            evacuate2(G - 1, (G - 1) % 2)
            square_root(2)
            act.wait_ge(bn_ready, 2)

            def normalise2(r):
                a2r = a2[:, bass.ds(r * 2, 2), :]
                nc.scalar.activation(a2r, a2r, ACT.Relu, bias=shift2[:, 0:1], scale=scale2[:, 0:1]).then_inc(a2_ready, 1)

            def evacuate3(tile, r, s):
                act.wait_ge(conv3_done, tile * R + r + 1)
                nc.scalar.activation(y3p(tile % 2, r), ps[:, 2 * s:2 * s + 2, 0:N], ACT.Copy).then_inc(y3_ready, 1)

            def scale_tile(tile, r, done):
                nc.scalar.activation(y3p(tile, r), y3p(tile, r), ACT.Identity,
                                     scale=scale3[:, tile:tile + 1]).then_inc(done, 1)

            normalise2(0)
            normalise2(3)
            for r in range(SLOTS):
                evacuate3(0, r, r)
                normalise2(SLOTS + r)
            for r in range(SLOTS, R):
                evacuate3(0, r, r % SLOTS)

            for r in range(3):
                evacuate3(1, r, r)
            square_root(3)
            evacuate3(1, 3, 3)
            act.wait_ge(bn_ready, 3)
            scale_tile(0, 0, scaled0)
            for r in range(SLOTS, R):
                evacuate3(1, r, r % SLOTS)
                if r < R - 1:
                    scale_tile(0, 2 * (r - SLOTS + 1), scaled0)

            def evacuate3_tile2(r):
                if r % 2 == 0:
                    act.wait_ge(added0, r // 2 + 1)
                else:
                    act.wait_ge(applied0, r // 2 + 1)
                evacuate3(2, r, r % SLOTS)

            def evacuate3_tile3(r):
                act.wait_ge(added1, r + 1)
                evacuate3(3, r, r % SLOTS)

            for r in range(SLOTS):
                evacuate3_tile2(r)
            square_root(4)
            act.wait_ge(bn_ready, 4)
            for r in range(SLOTS, R):
                scale_tile(1, r - SLOTS, scaled1)
                evacuate3_tile2(r)

            for r in range(SLOTS):
                scale_tile(1, r + SLOTS, scaled1)
                evacuate3_tile3(r)
                if r == 0:
                    square_root(5)
            for r in range(SLOTS, R):
                evacuate3_tile3(r)
            act.wait_ge(tile2_applied, 1)
            act.wait_ge(conv3_done, CT * R)
            for c in range(3):
                nc.scalar.activation(x[:, 0, c, :], x[:, 0, c, :], ACT.Relu, bias=shift3[:, c:c + 1]).then_inc(x1_relu, 1)
                act.wait_ge(x1_relu, c + 1)
                nc.scalar.activation(xs1[0][0][:, c, :], x[:, 0, c, :], ACT.Copy).then_inc(first_h, 1)
            square_root(6)
            for c in range(2):
                nc.scalar.activation(x[:, 1, c, :], x[:, 1, c, :], ACT.Relu, bias=shift3[:, c:c + 1]).then_inc(x1_relu, 1)

            def split_high1(g, s):
                act.wait_ge(x1_ready, g)
                need(act, bconv1_done, g - 1)
                nc.scalar.activation(xs1[s][0][:, :, :], xg(g), ACT.Copy).then_inc(x1h_ready, 1)

            def t1_high(g, s):
                act.wait_ge(bconv1_done, g + 1)
                need(act, bconv2_done, g - 1)
                nc.scalar.activation(inner(pads[s][0]), pixels(ps[:, s, 0:N]), ACT.Identity, bias=bias_t1[:, 0:1]).then_inc(t1h_ready, 1)

            def t2_high(g, s):
                act.wait_ge(bconv2_done, g + 1)
                need(act, bconv3_done, g - 1)
                nc.scalar.activation(t2[s][0][:, :], ps[:, 2 + s, 0:N], ACT.Identity, bias=bias_t2[:, 0:1]).then_inc(t2h_ready, 1)

            def finish(g):
                act.wait_ge(sum_ready, g + 1)
                nc.scalar.activation(xg(g), xg(g), ACT.Relu, bias=bias_y[:, 0:1]).then_inc(y_ready, 1)

            act.wait_ge(x1_first, 1)
            nc.scalar.activation(xs1[0][0][:, 3, :], x[:, 0, 3, :], ACT.Copy).then_inc(last_h, 1)
            t1_high(0, 0)
            split_high1(1, 1)
            t2_high(0, 0)
            split_high1(2, 0)
            t1_high(1, 1)
            finish(0)
            t2_high(1, 1)
            with act.Fori(1, (G - 2) // 2) as r:
                for s in range(2):
                    g = r * 2 + s
                    split_high1(g + 1, 1 - s)
                    t1_high(g, s)
                    finish(g - 1)
                    t2_high(g, s)
            split_high1(G - 1, 1)
            t1_high(G - 2, 0)
            finish(G - 3)
            t2_high(G - 2, 0)
            t1_high(G - 1, 1)
            finish(G - 2)
            t2_high(G - 1, 1)
            for c in range(CT):
                act.wait_ge(last_sum, c + 1)
                nc.scalar.activation(x[:, G - 1, c, :], x[:, G - 1, c, :], ACT.Relu, bias=bias_y[:, 0:1]).then_inc(y_ready, 1)

        @block.vector
        def _(dve):
            steps = [0]

            def chain(instruction):
                steps[0] += 1
                instruction.then_inc(dve_done, 1)
                dve.wait_ge(dve_done, steps[0])

            nc.vector.memset(warm[:, :], 0.0).then_inc(warm_ready, 1)
            nc.vector.memset(one[:, :], 1.0).then_inc(one_ready, 1)
            dve.wait_ge(w1h_ready, 1)
            nc.vector.tensor_tensor(wl[:, 0:CT], stage[:, 0:CT], wh[:, 0:CT].bitcast(F32), ALU.subtract).then_inc(w1l_ready, 1)

            def split_low(g, s):
                dve.wait_ge(xh_ready, g)
                nc.vector.tensor_tensor(xs0[s][1][:, 0:CT - 1, :], xg(g)[:, 0:CT - 1, :], xs0[s][0][:, 0:CT - 1, :].bitcast(F32),
                                        ALU.subtract).then_inc(xl_ready, 1)

            def gather(half, g, y, ready, count):
                dve.wait_ge(ready, count)
                nc.vector.bn_stats(stats[:, half, bass.ds(g, 1), :].rearrange("p a n -> p (a n)"), y).then_inc(stats_done, 1)

            for c in range(CT):
                dve.wait_ge(x0h_ready, c + 1)
                nc.vector.tensor_tensor(xs0[0][1][:, c, :], x[:, 0, c, :], xs0[0][0][:, c, :].bitcast(F32), ALU.subtract).then_inc(x0l_ready, 1)
            dve.wait_ge(par_loaded, 32)
            for i, c in enumerate((G1, G2)):
                nc.vector.tensor_scalar(half_g[:, i:i + 1], par[:, c:c + 1], -0.5, None, ALU.mult).then_inc(half_ready, 1)
            split_low(1, 1)
            for g in range(XS - 2):
                split_low(g + 2, g + 2)
                gather(0, g, y3g(0, g), y1_ready, g + 1)
            with dve.Fori(1, G // XS - 1) as r:
                for s in range(XS):
                    split_low(r * XS + s, s)
                    gather(0, r * XS + s - 2, y3g(0, r * XS + s - 2), y1_ready, r * XS + s - 1)
            for s in range(XS - 1):
                split_low(G - XS + s, s)
                gather(0, G - XS + s - 2, y3g(0, G - XS + s - 2), y1_ready, G - XS + s - 1)
            for c in range(CT):
                dve.wait_ge(x15h_ready, c + 1)
                nc.vector.tensor_tensor(xs0[XS - 1][1][:, c, :], x[:, G - 1, c, :], xs0[XS - 1][0][:, c, :].bitcast(F32),
                                        ALU.subtract).then_inc(x15l_ready, 1)
            for g in range(G - 3, G):
                gather(0, g, y3g(0, g), y1_ready, g + 1)

            def batch_norm(n, buffer, bias, half_gamma, beta, scale, shift, meanwhile=None):
                meanwhile = meanwhile or (lambda k: None)
                chain(nc.vector.bn_aggr(mv[:, :], stats[:, buffer].rearrange("p g s -> p (g s)")))
                nc.vector.tensor_scalar(var_eps[:, :], mv[:, 1:2], EPS, None, ALU.add).then_inc(var_ready, 1)
                nc.vector.scalar_tensor_tensor(mean_off[:, :], mv[:, 0:1], bias, bias, ALU.add, ALU.subtract).then_inc(mean_ready, 1)
                meanwhile(0)
                meanwhile(1)
                dve.wait_ge(std_ready, n)
                chain(nc.vector.reciprocal(r0[:, :], std[:, :]))
                nc.vector.tensor_tensor(gr[:, :], r0[:, :], half_gamma, ALU.mult)
                last = nc.vector.scalar_tensor_tensor(vrr[:, :], r0[:, :], var_eps[:, :], r0[:, :], ALU.mult, ALU.mult)
                steps[0] += 1
                last.then_inc(dve_done, 1)
                meanwhile(2)
                dve.wait_ge(dve_done, steps[0])
                last = nc.vector.scalar_tensor_tensor(scale, vrr[:, :], -3.0, gr[:, :], ALU.add, ALU.mult)
                steps[0] += 1
                last.then_inc(dve_done, 1)
                meanwhile(3)
                dve.wait_ge(dve_done, steps[0])
                dve.wait_ge(mean_ready, n)
                nc.vector.scalar_tensor_tensor(shift, mean_off[:, :], scale, beta, ALU.mult, ALU.subtract, reverse1=True).then_inc(bn_ready, 1)
                dve.wait_ge(bn_ready, n)

            def col(c, w=1):
                return par[:, c:c + w]

            dve.wait_ge(half_ready, 2)
            dve.wait_ge(stats_done, G)
            batch_norm(1, 0, col(B1), half_g[:, 0:1], col(BE1), scale1[:, :], shift1[:, :])

            def split1(g, s):
                need(dve, conv2_done, g - 1)
                dve.wait_ge(a1_ready, g + 1)
                nc.vector.tensor_scalar(inner(pads[s][0]), pixels(y3g(0, g)), 1.0, None, ALU.mult).then_inc(padh_ready, 1)
                dve.wait_ge(padh_ready, g + 1)
                nc.vector.tensor_tensor(inner(pads[s][1]), pixels(y3g(0, g)), inner(pads[s][0]).bitcast(F32), ALU.subtract).then_inc(padl_ready, 1)

            dve.wait_ge(pads_zero, 1)
            split1(0, 0)
            split1(1, 1)
            s_ = scal[:, RES_SCALE:RES_SCALE + 1]
            nc.vector.scalar_tensor_tensor(sp[:, 0:1], s_, -1.0, s_, ALU.mult, ALU.max).then_inc(sp_ready, 1)
            dve.wait_ge(sp_exp, 1)
            nc.vector.tensor_scalar(sp[:, 2:3], sp[:, 1:2], 1.0, None, ALU.add).then_inc(sp_ready, 1)
            dve.wait_ge(sp_ready, 2)
            chain(nc.vector.tensor_scalar(sp[:, 4:5], sp[:, 2:3], -1.0, TINY, ALU.add, ALU.add))
            chain(nc.vector.reciprocal(sp[:, 5:6], sp[:, 4:5]))
            dve.wait_ge(sp_log, 1)
            chain(nc.vector.scalar_tensor_tensor(sp[:, 6:7], sp[:, 3:4], TINY, sp[:, 5:6], ALU.add, ALU.mult))
            chain(nc.vector.tensor_tensor(sp[:, 4:5], sp[:, 6:7], sp[:, 1:2], ALU.mult))
            chain(nc.vector.scalar_tensor_tensor(sp[:, 7:8], s_, 0.0, sp[:, 4:5], ALU.max, ALU.add))
            nc.vector.tensor_scalar(g3s[:, :], par[:, G3:G3 + CT], sp[:, 7:8], None, ALU.mult)
            chain(nc.vector.tensor_scalar(be3s[:, :], par[:, BE3:BE3 + CT], sp[:, 7:8], None, ALU.mult))
            chain(nc.vector.tensor_scalar(half_g[:, 2:2 + CT], g3s[:, :], -0.5, None, ALU.mult))

            def sc(c):
                return scal[:, c:c + 1]
            nc.vector.tensor_tensor(bias_t1[:, :], sc(BIAS1B), sc(BIAS2A), ALU.add)
            nc.vector.tensor_tensor(bias_t2[:, :], sc(BIAS2B), sc(BIAS3A), ALU.add)
            chain(nc.vector.scalar_tensor_tensor(bias_y[:, :], sc(BIAS3B), sc(RSCALE), sc(RBIAS), ALU.mult, ALU.add))

            gather(0, 0, a2g(0), y2_ready, 1)
            with dve.Fori(1, G // 2) as r:
                for s in range(2):
                    split1(r * 2 + s, s)
                    gather(0, r * 2 + s - 1, a2g(r * 2 + s - 1), y2_ready, r * 2 + s)
            gather(0, G - 1, a2g(G - 1), y2_ready, G)
            dve.wait_ge(stats_done, 2 * G)
            batch_norm(2, 0, col(B2), half_g[:, 1:2], col(BE2), scale2[:, :], shift2[:, :])

            def gather3(tile, r, i):
                if i == 0:
                    dve.wait_ge(y3_ready, tile * R + r + 1)
                g = r * 2 + i
                nc.vector.bn_stats(stats[:, tile % 2, bass.ds(g, 1), :].rearrange("p a n -> p (a n)"), y3g(tile % 2, g)).then_inc(stats_done, 1)

            def norm3(tile, meanwhile=None):
                dve.wait_ge(stats_done, (3 + tile) * G)
                batch_norm(3 + tile, tile % 2, col(B3 + tile), half_g[:, 2 + tile:3 + tile], be3s[:, tile:tile + 1],
                           scale3[:, tile:tile + 1], shift3[:, tile:tile + 1], meanwhile)

            def apply(g, c):
                return nc.vector.scalar_tensor_tensor(xt(g, c), y3g(c % 2, g), scale3[:, c:c + 1], xt(g, c), ALU.mult, ALU.add)

            def apply_tile0(r):
                nc.vector.scalar_tensor_tensor(xp(r, 0), y3p(0, r), scale3[:, 0:1], xp(r, 0), ALU.mult, ALU.add).then_inc(applied0, 1)

            for r in (1, 2):
                nc.vector.tensor_scalar(a2[:, 2 * r:2 * r + 2, :], a2[:, 2 * r:2 * r + 2, :], scale2[:, 0:1], shift2[:, 0:1],
                                        ALU.mult, ALU.add).then_inc(a2_scaled, 1)
                dve.wait_ge(a2_scaled, r)
                nc.vector.tensor_scalar(a2[:, 2 * r:2 * r + 2, :], a2[:, 2 * r:2 * r + 2, :], 0.0, None, ALU.max).then_inc(a2b_ready, 1)
            with dve.Fori(0, R) as r:
                for i in range(2):
                    gather3(0, r, i)
            norm3(0, lambda k: gather3(1, k // 2, k % 2))
            apply_tile0(1)
            with dve.Fori(1, R // 2) as k:
                for j in range(2):
                    for i in range(2):
                        gather3(1, k * 2 + j, i)
                apply_tile0(k * 2 + 1)
            norm3(1, lambda k: gather3(2, k // 2, k % 2))
            with dve.Fori(2, R) as r:
                for i in range(2):
                    gather3(2, r, i)
            norm3(2, lambda k: gather3(3, k // 2, k % 2))
            apply(0, 2).then_inc(tile2_applied, 1)
            with dve.Fori(2, R) as r:
                for i in range(2):
                    gather3(3, r, i)
            norm3(3)

            def block0_result(g):
                apply(g, 2)
                apply(g, 3).then_inc(x1_part, 1)
                for c in range(CT):
                    if c == 2:
                        dve.wait_ge(x1_part, g - 1)
                    last = nc.vector.tensor_scalar(xt(g, c), xt(g, c), shift3[:, c:c + 1], 0.0, ALU.add, ALU.max)
                last.then_inc(x1_ready, 1)

            def split_low1(g, s):
                dve.wait_ge(x1h_ready, g)
                nc.vector.tensor_tensor(xs1[s][1][:, :, :], xg(g), xs1[s][0][:, :, :].bitcast(F32), ALU.subtract).then_inc(x1l_ready, 1)

            def t1_low(g, s):
                dve.wait_ge(t1h_ready, g + 1)
                nc.vector.scalar_tensor_tensor(inner(pads[s][1]), pixels(ps[:, s, 0:N]), bias_t1[:, 0:1], inner(pads[s][0]).bitcast(F32),
                                               ALU.add, ALU.subtract).then_inc(t1l_ready, 1)

            def t2_low(g, s):
                dve.wait_ge(t2h_ready, g + 1)
                nc.vector.scalar_tensor_tensor(t2[s][1][:, :], ps[:, 2 + s, 0:N], bias_t2[:, 0:1], t2[s][0][:, :].bitcast(F32),
                                               ALU.add, ALU.subtract).then_inc(t2l_ready, 1)

            def add_result(g):
                dve.wait_ge(bconv3_done, g + 1)
                nc.vector.scalar_tensor_tensor(xg(g), ps[:, 4:8, 0:N], scal[:, RSCALE:RSCALE + 1], xg(g),
                                               ALU.mult, ALU.add).then_inc(sum_ready, 1)

            chain(apply(0, 3))
            nc.vector.tensor_scalar(xt(0, 3), xt(0, 3), shift3[:, 3:4], 0.0, ALU.add, ALU.max).then_inc(x1_first, 1)
            dve.wait_ge(last_h, 1)
            nc.vector.tensor_tensor(xs1[0][1][:, 3, :], x[:, 0, 3, :], xs1[0][0][:, 3, :].bitcast(F32), ALU.subtract).then_inc(last_l, 1)
            dve.wait_ge(added0, R // 2)
            dve.wait_ge(added1, R)
            apply(1, 2)
            chain(apply(1, 3))
            dve.wait_ge(x1_relu, 5)
            for c in (2, 3):
                last = nc.vector.tensor_scalar(xt(1, c), xt(1, c), shift3[:, c:c + 1], 0.0, ALU.add, ALU.max)
            last.then_inc(x1_ready, 1)
            t1_low(0, 0)
            split_low1(1, 1)
            block0_result(2)
            t2_low(0, 0)
            t1_low(1, 1)
            split_low1(2, 0)
            add_result(0)
            block0_result(3)
            t2_low(1, 1)
            with dve.Fori(1, (G - 2) // 2) as r:
                for s in range(2):
                    g = r * 2 + s
                    t1_low(g, s)
                    split_low1(g + 1, 1 - s)
                    add_result(g - 1)
                    block0_result(g + 2)
                    t2_low(g, s)
            t1_low(G - 2, 0)
            split_low1(G - 1, 1)
            add_result(G - 3)
            t2_low(G - 2, 0)
            t1_low(G - 1, 1)
            add_result(G - 2)
            t2_low(G - 1, 1)
            for c in range(CT):
                dve.wait_ge(bconv3_done, G + c)
                nc.vector.scalar_tensor_tensor(x[:, G - 1, c, :], ps[:, 4 + c, 0:N], scal[:, RSCALE:RSCALE + 1], x[:, G - 1, c, :],
                                               ALU.mult, ALU.add).then_inc(last_sum, 1)

        @block.tensor
        def _(pe):
            def products(bank, terms):
                passes = [p for t, vh, vl in terms for p in ((wh, t, vh), (wh, t, vl), (wl, t, vh))]
                for i, (w, t, v) in enumerate(passes):
                    last = nc.tensor.matmul(ps[:, bank, 0:N], w[:, t, :], v, start=i == 0, stop=i == len(passes) - 1)
                return last

            def taps(pad):
                return [pad[:, k // 3 * GI:(k // 3 + H) * GI, k % 3:k % 3 + W] for k in range(TAPS)]

            def conv_1x1(bank, split):
                return products(bank, [(W1 + c, split[0][:, c, :], split[1][:, c, :]) for c in range(CT)])

            def conv_3x3(bank, pad):
                return products(bank, [(W2 + k, h, l) for k, (h, l) in enumerate(zip(taps(pad[0]), taps(pad[1])))])

            def conv1(g, s):
                pe.wait_ge(xl_ready, g)
                pe.wait_ge(xl3_ready, g)
                need(pe, y1_ready, g - XS + 1)
                conv_1x1(s, xs0[s]).then_inc(conv1_done, 1)

            def products_1x1_by_tile(bank, split, ready, fill=0):
                for c in range(CT):
                    if fill and c in (0, 3):
                        keep_warm(fill, 1)
                    if ready[c]:
                        pe.wait_ge(*ready[c])
                    h, l = split[0][:, c, :], split[1][:, c, :]
                    for i, (w, v) in enumerate(((wh, h), (wh, l), (wl, h))):
                        last = nc.tensor.matmul(ps[:, bank, 0:N], w[:, W1 + c, :], v, start=c + i == 0, stop=c == CT - 1 and i == 2)
                return last

            def keep_warm(count, bank=BANKS - 1):
                for i in range(count):
                    nc.tensor.matmul(ps[:, bank, 0:N], warm[:, 0:P], warm[:, :], start=True, stop=True)

            pe.wait_ge(warm_ready, 1)
            keep_warm(10)
            pe.wait_ge(w1l_ready, 1)
            products_1x1_by_tile(0, xs0[0], [(x0l_ready, c + 1) for c in range(CT)]).then_inc(conv1_done, 1)
            for s in range(1, XS):
                conv1(s, s)
            with pe.Fori(1, G // XS - 1) as r:
                for s in range(XS):
                    conv1(r * XS + s, s)
            for s in range(XS - 1):
                conv1(G - XS + s, s)
            pe.wait_ge(y1_ready, G - XS)
            products_1x1_by_tile(XS - 1, xs0[XS - 1], [(x15l_ready, c + 1) for c in range(CT)]).then_inc(conv1_done, 1)
            keep_warm(28)

            def conv2(g, s):
                pe.wait_ge(padl_ready, g + 1)
                need(pe, y2_ready, g - 1)
                conv_3x3(s, pads[s]).then_inc(conv2_done, 1)

            pe.wait_ge(w2_ready, 1)
            for s in range(2):
                conv2(s, s)
            with pe.Fori(1, G // 2) as r:
                for s in range(2):
                    conv2(r * 2 + s, s)

            keep_warm(22)

            def conv3(tile, r, s):
                if tile == 0 and r in (1, 2):
                    pe.wait_ge(a2b_ready, r)
                elif tile == 0:
                    pe.wait_ge(a2_ready, 1 if r == 0 else r - 1)
                need(pe, y3_ready, tile * R + r - SLOTS + 1)
                for i in range(2):
                    last = nc.tensor.matmul(ps[:, 2 * s + i, 0:N], w3s[:, tile, :], a2g(r * 2 + i), start=True, stop=True)
                last.then_inc(conv3_done, 1)

            pe.wait_ge(w03_loaded, 16)
            for s in range(SLOTS):
                conv3(0, s, s)
            for s in range(SLOTS):
                conv3(0, SLOTS + s, s)
            for tile in range(1, CT):
                with pe.Fori(0, R // SLOTS) as k:
                    for s in range(SLOTS):
                        conv3(tile, k * SLOTS + s, s)

            def b_conv1(g, s):
                pe.wait_ge(x1l_ready, g)
                need(pe, t1l_ready, g - 1)
                conv_1x1(s, xs1[s]).then_inc(bconv1_done, 1)

            def b_conv2(g, s):
                pe.wait_ge(t1l_ready, g + 1)
                need(pe, t2l_ready, g - 1)
                conv_3x3(2 + s, pads[s]).then_inc(bconv2_done, 1)

            def b_conv3(g, s):
                pe.wait_ge(t2l_ready, g + 1)
                need(pe, sum_ready, g)
                for c in range(CT):
                    last = products(4 + c, [(W3 + c, t2[s][0][:, :], t2[s][1][:, :])])
                last.then_inc(bconv3_done, 1)

            pe.wait_ge(wb1_ready, 1)
            pe.wait_ge(y3_ready, CT * R - SLOTS + 1)
            products_1x1_by_tile(0, xs1[0], [(first_l, 1), (first_l, 2), (first_l, 3), (last_l, 1)], 12).then_inc(bconv1_done, 1)
            b_conv2(0, 0)
            pe.wait_ge(wb1c_ready, 1)
            b_conv1(1, 1)
            b_conv3(0, 0)
            b_conv2(1, 1)
            with pe.Fori(1, G // 2) as r:
                for s in range(2):
                    g = r * 2 + s
                    b_conv1(g, s)
                    b_conv3(g - 1, 1 - s)
                    b_conv2(g, s)
            pe.wait_ge(t2l_ready, G)
            pe.wait_ge(sum_ready, G - 1)
            for c in range(CT):
                products(4 + c, [(W3 + c, t2[1][0][:, :], t2[1][1][:, :])]).then_inc(bconv3_done, 1)


def kernel(x, L0_conv_w1, L0_conv_b1, L0_conv_g1, L0_conv_be1, L0_conv_w2, L0_conv_b2, L0_conv_g2, L0_conv_be2,
           L0_conv_w3, L0_conv_b3, L0_conv_g3, L0_conv_be3, L0_conv_residual_scale, L1_conv_w1, L1_conv_w2,
           L1_conv_w3, L1_conv_bias1b, L1_conv_bias2a, L1_conv_bias2b, L1_conv_bias3a, L1_conv_bias3b,
           L1_conv_rscale, L1_conv_rbias):
    import numpy as np
    import concourse.bacc as bacc
    from concourse.bass_utils import run_bass_kernel_spmd

    def weights(w1, w2, w3):
        a = np.asarray(w1).reshape(P, CT, P).transpose(2, 1, 0)
        b = np.asarray(w2).reshape(P, P, TAPS).transpose(1, 2, 0)
        c = np.asarray(w3).reshape(CT, P, P).transpose(2, 0, 1)
        return np.ascontiguousarray(np.concatenate([a, b, c], axis=1))

    def columns(*vectors):
        return np.ascontiguousarray(np.concatenate([np.asarray(v).reshape(-1, P).T for v in vectors], axis=1))

    arrays = {
        "x_dram": np.ascontiguousarray(np.asarray(x).reshape(G, GI, CT, P, H, W).transpose(3, 0, 2, 4, 1, 5)).reshape(P, G, CT, N),
        "w0_dram": weights(L0_conv_w1, L0_conv_w2, L0_conv_w3),
        "w1_dram": weights(L1_conv_w1, L1_conv_w2, L1_conv_w3),
        "par_dram": columns(L0_conv_b1, L0_conv_g1, L0_conv_be1, L0_conv_b2, L0_conv_g2, L0_conv_be2,
                            L0_conv_b3, L0_conv_g3, L0_conv_be3),
        "scal_dram": np.concatenate([np.asarray(v) for v in (
            L0_conv_residual_scale, L1_conv_rscale, L1_conv_rbias, L1_conv_bias1b, L1_conv_bias2a,
            L1_conv_bias2b, L1_conv_bias3a, L1_conv_bias3b)]),
    }
    nc = bacc.Bacc("TRN2", target_bir_lowering=False, num_devices=1)
    args = [nc.dram_tensor(n, a.shape, mybir.dt.from_np(a.dtype), kind="ExternalInput").ap() for n, a in arrays.items()]
    out = nc.dram_tensor("out_dram", (P, G, CT, N), F32, kind="ExternalOutput").ap()
    build(nc, *args, out)
    r = run_bass_kernel_spmd(nc, [arrays], core_ids=[0])
    y = r.results[0]["out_dram"].reshape(P, G, CT, H, GI, W).transpose(1, 4, 2, 0, 3, 5)
    return np.ascontiguousarray(y).reshape(IMAGES, CHANNELS, H, W)
```

```python
from contextlib import ExitStack

import concourse.bass as bass
from concourse import mybir

F32 = mybir.dt.float32
F32R = mybir.dt.float32r
ALU = mybir.AluOpType
ACT = mybir.ActivationFunctionType

P = 128
IMAGES, CHANNELS, H, W = 32, 512, 14, 14
CT = CHANNELS // P
GI = 2
G = IMAGES // GI
N = GI * H * W
TAPS = 9
W1, W2, W3 = 0, CT, CT + TAPS
WT = CT + TAPS + CT
W12 = CT + TAPS
BANK = 512
BANKS = 8
EPS = 1e-5
TINY = 1e-30
XQ = 4
XS = 4

B1, G1, BE1, B2, G2, BE2, B3, G3, BE3, NPAR = 0, 1, 2, 3, 4, 5, 6, 10, 14, 18
RES_SCALE, RSCALE, RBIAS, BIAS1B, BIAS2A, BIAS2B, BIAS3A, BIAS3B, NSC = 0, 1, 2, 3, 4, 5, 6, 7, 8


def need(engine, sem, value):
    if isinstance(value, int) and value <= 0:
        return
    engine.wait_ge(sem, value)


def build(nc, x_in, w0_in, w1_in, par_in, scal_in, out):
    with ExitStack() as ctx:
        at = -(-nc.sbuf_base // 32) * 32

        def region(size):
            nonlocal at
            start = at
            at += size
            return start

        x_at = region(4 * G * CT * N)
        y_at = region(4 * 2 * G * N)
        a_at = region(4 * G * N)
        stage_at = region(4 * W12 * P)
        wh_at = region(4 * WT * P)
        wl_at = region(4 * WT * P)
        w3_at = region(4 * CT * P)
        t1_at = region(2 * 2 * 4 * N)
        small_at = region(2600)

        def place(name, shape, dtype, offset):
            return nc.alloc_sbuf_tensor_at(name, shape, dtype, offset=offset)

        x = place("x", [P, G, CT, N], F32, x_at)
        y3 = place("y3", [P, 2, G, N], F32, y_at)
        a2 = place("a2", [P, G, N], F32, a_at)
        XB = 4 * CT * N
        xs0 = [(place(f"xh0_{s}", [P, CT, N], F32R, y_at + 4 * G * N + 2 * s * XB),
                place(f"xl0_{s}", [P, CT, N], F32R, y_at + 4 * G * N + (2 * s + 1) * XB)) for s in range(XS)]
        xs1 = [(place(f"xh1_{s}", [P, CT, N], F32R, a_at + 2 * s * XB),
                place(f"xl1_{s}", [P, CT, N], F32R, a_at + (2 * s + 1) * XB)) for s in range(2)]
        stage = place("stage", [P, W12, P], F32, stage_at)
        t2 = [(place(f"t2h_{s}", [P, N], F32R, stage_at + 8 * s * N),
               place(f"t2l_{s}", [P, N], F32R, stage_at + 8 * s * N + 4 * N)) for s in range(2)]
        wh = place("wh", [P, WT, P], F32R, wh_at)
        wl = place("wl", [P, WT, P], F32R, wl_at)
        w3s = place("w3s", [P, CT, P], F32, w3_at)
        t1 = [(place(f"t1h_{s}", [P, N], F32R, t1_at + 2 * s * 4 * N),
               place(f"t1l_{s}", [P, N], F32R, t1_at + (2 * s + 1) * 4 * N)) for s in range(2)]

        def small(name, *shape):
            nonlocal small_at
            n = 1
            for d in shape:
                n *= d
            t = place(name, [P, *shape], F32, small_at)
            small_at += 32 * -(-4 * n // 32)
            return t

        par = small("par", NPAR)
        scal = small("scal", NSC)
        stats = small("stats", 2, G, 6)
        mv = small("mv", 2)
        scale1, shift1 = small("scale1", 1), small("shift1", 1)
        scale2, shift2 = small("scale2", 1), small("shift2", 1)
        scale3, shift3 = small("scale3", CT), small("shift3", CT)
        g3s, be3s = small("g3s", CT), small("be3s", CT)
        one = small("one", 1)
        warm = place("warm", [P, N], mybir.dt.bfloat16, small_at)
        small_at += 32 * -(-2 * N // 32)
        var_eps, std, r0, vrr, gr, mean_off = (small(n, 1) for n in ("var_eps", "std", "r0", "vrr", "gr", "mean_off"))
        half_g = small("half_g", 2 + CT)
        sp = small("sp", 8)
        bias_t1, bias_t2, bias_y = small("bias_t1", 1), small("bias_t2", 1), small("bias_y", 1)
        assert small_at <= at and small_at <= nc.sbuf_usable_end

        ps = ctx.enter_context(nc.psum_tensor("ps", [P, BANKS, BANK], F32))

        def sem(name):
            return ctx.enter_context(nc.semaphore(name))

        x0_loaded = [sem(f"x0_loaded{c}") for c in range(CT)]
        x0h_ready, x0l_ready = sem("x0h_ready"), sem("x0l_ready")
        w03_loaded = sem("w03_loaded")
        mean_ready, a2_scaled, a2b_ready = sem("mean_ready"), sem("a2_scaled"), sem("a2b_ready")
        vector_scaled1 = sem("vector_scaled1")
        one_ready, half_ready, warm_ready = sem("one_ready"), sem("half_ready"), sem("warm_ready")
        xl3_ready, w2h_ready = sem("xl3_ready"), sem("w2h_ready")
        x15h_ready, x15l_ready = sem("x15h_ready"), sem("x15l_ready")
        scaled0, scaled1, x1_first, first_h, first_l = (
            sem(n) for n in ("scaled0", "scaled1", "x1_first", "first_h", "first_l"))
        x1_relu, last_h, last_l, tile2_applied = (sem(n) for n in ("x1_relu", "last_h", "last_l", "tile2_applied"))
        last_sum = sem("last_sum")
        x_loaded = [sem(f"x_loaded{i}") for i in range(XQ)]
        par_loaded, w0_loaded, w0b_loaded, w1_loaded, w1c_loaded = (
            sem(n) for n in ("par_loaded", "w0_loaded", "w0b_loaded", "w1_loaded", "w1c_loaded"))
        out_stored = sem("out_stored")
        dve_done = sem("dve_done")
        pool_done = sem("pool_done")
        sp_ready, sp_exp, sp_log = sem("sp_ready"), sem("sp_exp"), sem("sp_log")
        w1h_ready, w1l_ready, w2_ready, wb1_ready, wb1c_ready = (
            sem(n) for n in ("w1h_ready", "w1l_ready", "w2_ready", "wb1_ready", "wb1c_ready"))
        xh_ready, xl_ready, conv1_done, y1_ready = (sem(n) for n in ("xh_ready", "xl_ready", "conv1_done", "y1_ready"))
        a1_ready, a1l_ready, conv2_done, y2_ready = (sem(n) for n in ("a1_ready", "a1l_ready", "conv2_done", "y2_ready"))
        stats_done = sem("stats_done")
        var_ready, std_ready, bn_ready = sem("var_ready"), sem("std_ready"), sem("bn_ready")
        a2_ready, conv3_done, y3_ready, applied0, added0, added1 = (
            sem(n) for n in ("a2_ready", "conv3_done", "y3_ready", "applied0", "added0", "added1"))
        x1_ready, x1h_ready, x1l_ready, bconv1_done = (sem(n) for n in ("x1_ready", "x1h_ready", "x1l_ready", "bconv1_done"))
        t1h_ready, t1l_ready, bconv2_done = sem("t1h_ready"), sem("t1l_ready"), sem("bconv2_done")
        x1_part, a1h_ready = sem("x1_part"), sem("a1h_ready")
        t2h_ready, t2l_ready, bconv3_done = sem("t2h_ready"), sem("t2l_ready"), sem("bconv3_done")
        sum_ready, y_ready = sem("sum_ready"), sem("y_ready")

        block = ctx.enter_context(nc.Block())

        def rows(ap):
            return ap.rearrange("p (r w) -> p r w", w=GI * W)

        def xg(g):
            return x[:, bass.ds(g, 1), :, :].rearrange("p a c n -> p (a c) n")

        def xt(g, c):
            return x[:, bass.ds(g, 1), c, :].rearrange("p a n -> p (a n)")

        def a2g(g):
            return a2[:, bass.ds(g, 1), :].rearrange("p a n -> p (a n)")

        def y3g(half, g):
            return y3[:, half, bass.ds(g, 1), :].rearrange("p a n -> p (a n)")

        def y3p(half, r):
            return y3[:, half, bass.ds(r * 2, 2), :]

        def xp(r, c):
            return x[:, bass.ds(r * 2, 2), c, :]

        R = G // 2
        SLOTS = BANKS // 2
        VECTOR_PAIRS = tuple(range(3, R, 2))
        SCALAR_PAIRS = tuple(r for r in range(R) if r not in VECTOR_PAIRS)

        @block.sync
        def _(sync):
            def load_x(g, s):
                sync.dma_start(xg(g), x_in[:, bass.ds(g, 1), :, :].rearrange("p a c n -> p (a c) n")).then_inc(x_loaded[s], 16)

            sync.dma_start(stage[:, 0:CT], w0_in[:, 0:CT]).then_inc(w0_loaded, 16)
            for c in range(CT):
                sync.dma_start(x[:, 0, c, :], x_in[:, 0, c, :]).then_inc(x0_loaded[c], 16)
            for g in range(1, XQ):
                load_x(g, g)
            for c in range(CT):
                sync.wait_ge(x0_loaded[c], 16)
            load_x(XQ, 0)
            with sync.Fori(1, G // XQ - 1) as r:
                for s in range(1, XQ + 1):
                    sync.wait_ge(x_loaded[s % XQ], r * 16)
                    load_x(r * XQ + s, s % XQ)
            for s in range(1, XQ):
                sync.wait_ge(x_loaded[s], (G // XQ - 1) * 16)
                load_x(G - XQ + s, s)
            sync.dma_start(stage[:, CT:W12], w0_in[:, CT:W12]).then_inc(w0b_loaded, 16)
            sync.dma_start(w3s[:, :, :], w0_in[:, W3:WT]).then_inc(w03_loaded, 16)
            sync.wait_ge(w1l_ready, 1)
            sync.wait_ge(w2_ready, 1)
            sync.dma_start(stage[:, :, :], w1_in[:, 0:W12]).then_inc(w1_loaded, 16)
            sync.wait_ge(conv3_done, CT * R)
            sync.dma_start(w3s[:, :, :], w1_in[:, W3:WT]).then_inc(w1c_loaded, 16)
            with sync.Fori(0, G - 1) as g:
                sync.wait_ge(y_ready, g + 1)
                sync.dma_start(out[:, bass.ds(g, 1), :, :].rearrange("p a c n -> p (a c) n"), xg(g)).then_inc(out_stored, 16)
            for c in range(CT):
                sync.wait_ge(y_ready, G + c)
                sync.dma_start(out[:, G - 1, c, :], x[:, G - 1, c, :]).then_inc(out_stored, 16)
            sync.wait_ge(out_stored, 16 * (G - 1 + CT))

        @block.gpsimd
        def _(pool):
            def split_low3(g, s):
                pool.wait_ge(xh_ready, g)
                nc.gpsimd.tensor_tensor(xs0[s][1][:, CT - 1, :], xt(g, CT - 1), xs0[s][0][:, CT - 1, :].bitcast(F32), ALU.subtract).then_inc(xl3_ready, 1)

            for s in range(1, XS):
                split_low3(s, s)
            with pool.Fori(1, G // XS - 1) as r:
                for s in range(XS):
                    split_low3(r * XS + s, s)
            for s in range(XS - 1):
                split_low3(G - XS + s, s)
            pool.wait_ge(w2h_ready, 1)
            nc.gpsimd.tensor_tensor(wl[:, W2:W12], stage[:, W2:W12], wh[:, W2:W12].bitcast(F32), ALU.subtract).then_inc(w2_ready, 1)
            pool.wait_ge(w1_loaded, 16)
            pool.wait_ge(conv2_done, G)
            nc.gpsimd.tensor_copy(wh[:, 0:W12], stage[:, :, :]).then_inc(pool_done, 1)
            pool.wait_ge(pool_done, 1)
            nc.gpsimd.tensor_tensor(wl[:, 0:W12], stage[:, :, :], wh[:, 0:W12].bitcast(F32), ALU.subtract).then_inc(wb1_ready, 1)
            with pool.Fori(0, R // 2) as k:
                pool.wait_ge(scaled0, k + 1)
                nc.gpsimd.tensor_tensor(xp(k * 2, 0), xp(k * 2, 0), y3p(0, k * 2), ALU.add).then_inc(added0, 1)
            for r in range(R):
                if r in VECTOR_PAIRS:
                    pool.wait_ge(vector_scaled1, VECTOR_PAIRS.index(r) + 1)
                else:
                    pool.wait_ge(scaled1, SCALAR_PAIRS.index(r) + 1)
                nc.gpsimd.tensor_tensor(xp(r, 1), xp(r, 1), y3p(1, r), ALU.add).then_inc(added1, 1)
            for c in range(3):
                pool.wait_ge(first_h, c + 1)
                nc.gpsimd.tensor_tensor(xs1[0][1][:, c, :], x[:, 0, c, :], xs1[0][0][:, c, :].bitcast(F32), ALU.subtract).then_inc(first_l, 1)
            pool.wait_ge(w1c_loaded, 16)
            nc.gpsimd.tensor_copy(wh[:, W3:WT], w3s[:, :, :]).then_inc(pool_done, 1)
            pool.wait_ge(pool_done, 2)
            nc.gpsimd.tensor_tensor(wl[:, W3:WT], w3s[:, :, :], wh[:, W3:WT].bitcast(F32), ALU.subtract).then_inc(wb1c_ready, 1)

        @block.scalar
        def _(act):
            act.dma_start(par[:, :], par_in).then_inc(par_loaded, 16)
            act.dma_start(scal[:, :], scal_in.rearrange("(a n) -> a n", a=1).to_broadcast([P, NSC])).then_inc(par_loaded, 16)
            act.wait_ge(one_ready, 1)
            nc.scalar.activation(std[:, 0:1], one[:, 0:1], ACT.Sqrt)
            act.wait_ge(w0_loaded, 16)
            nc.scalar.activation(wh[:, 0:CT], stage[:, 0:CT], ACT.Copy).then_inc(w1h_ready, 1)

            def split_high(g, s, r):
                act.wait_ge(x_loaded[s], 16 * (r + (0 if s == 0 else 1)))
                need(act, conv1_done, g - XS + 1)
                nc.scalar.activation(xs0[s][0][:, :, :], xg(g), ACT.Copy).then_inc(xh_ready, 1)

            def evacuate1(g, s):
                act.wait_ge(conv1_done, g + 1)
                nc.scalar.activation(y3g(0, g), ps[:, s, 0:N], ACT.Copy).then_inc(y1_ready, 1)

            for c in range(CT):
                act.wait_ge(x0_loaded[c], 16)
                nc.scalar.activation(xs0[0][0][:, c, :], x[:, 0, c, :], ACT.Copy).then_inc(x0h_ready, 1)
            split_high(1, 1, 0)
            for g in range(XS - 2):
                split_high(g + 2, g + 2, 0)
                evacuate1(g, g)
            with act.Fori(1, G // XS - 1) as r:
                for s in range(XS):
                    split_high(r * XS + s, s, r)
                    evacuate1(r * XS + s - 2, (s - 2) % XS)
            for s in range(XS - 1):
                split_high(G - XS + s, s, G // XS - 1)
                evacuate1(G - XS + s - 2, (s - 2) % XS)
            act.wait_ge(x_loaded[XS - 1], 16 * (G // XS))
            act.wait_ge(conv1_done, G - XS)
            for c in range(CT):
                nc.scalar.activation(xs0[XS - 1][0][:, c, :], x[:, G - 1, c, :], ACT.Copy).then_inc(x15h_ready, 1)
            for g in range(G - 3, G - 1):
                evacuate1(g, g % XS)
            act.wait_ge(w0b_loaded, 16)
            nc.scalar.activation(wh[:, W2:W12], stage[:, W2:W12], ACT.Copy).then_inc(w2h_ready, 1)

            def square_root(n):
                act.wait_ge(var_ready, n)
                nc.scalar.activation(std[:, :], var_eps[:, :], ACT.Sqrt).then_inc(std_ready, 1)

            square_root(1)
            evacuate1(G - 1, XS - 1)
            act.wait_ge(bn_ready, 1)
            act.wait_ge(y1_ready, G)

            def normalise1(g):
                nc.scalar.activation(y3g(0, g), y3g(0, g), ACT.Relu, bias=shift1[:, 0:1], scale=scale1[:, 0:1]).then_inc(a1_ready, 1)

            def evacuate2(g, s):
                act.wait_ge(conv2_done, g + 1)
                nc.scalar.activation(a2g(g), ps[:, s, 0:N], ACT.Copy).then_inc(y2_ready, 1)

            normalise1(0)
            normalise1(1)
            act.wait_ge(sp_ready, 1)
            nc.scalar.activation(sp[:, 1:2], sp[:, 0:1], ACT.Exp, scale=-1.0).then_inc(sp_exp, 1)
            act.wait_ge(sp_ready, 2)
            nc.scalar.activation(sp[:, 3:4], sp[:, 2:3], ACT.Ln).then_inc(sp_log, 1)
            nc.scalar.activation(std[:, 0:1], one[:, 0:1], ACT.Sqrt)
            evacuate2(0, 0)
            with act.Fori(1, G // 2) as r:
                for s in range(2):
                    normalise1(r * 2 + s)
                    evacuate2(r * 2 + s - 1, (s - 1) % 2)
            square_root(2)
            evacuate2(G - 1, (G - 1) % 2)
            act.wait_ge(bn_ready, 2)
            act.wait_ge(y2_ready, G)

            def normalise2(r):
                a2r = a2[:, bass.ds(r * 2, 2), :]
                nc.scalar.activation(a2r, a2r, ACT.Relu, bias=shift2[:, 0:1], scale=scale2[:, 0:1]).then_inc(a2_ready, 1)

            def evacuate3(tile, r, s):
                act.wait_ge(conv3_done, tile * R + r + 1)
                nc.scalar.activation(y3p(tile % 2, r), ps[:, 2 * s:2 * s + 2, 0:N], ACT.Copy).then_inc(y3_ready, 1)

            def scale_tile(tile, r, done):
                nc.scalar.activation(y3p(tile, r), y3p(tile, r), ACT.Identity,
                                     scale=scale3[:, tile:tile + 1]).then_inc(done, 1)

            normalise2(0)
            normalise2(3)
            for r in range(SLOTS):
                evacuate3(0, r, r)
                normalise2(SLOTS + r)
            for r in range(SLOTS, R):
                evacuate3(0, r, r % SLOTS)

            for r in range(3):
                evacuate3(1, r, r)
            square_root(3)
            evacuate3(1, 3, 3)
            act.wait_ge(bn_ready, 3)
            scale_tile(0, 0, scaled0)
            for r in range(SLOTS, R):
                evacuate3(1, r, r % SLOTS)
                if r < R - 1:
                    scale_tile(0, 2 * (r - SLOTS + 1), scaled0)

            def evacuate3_tile2(r):
                if r % 2 == 0:
                    act.wait_ge(added0, r // 2 + 1)
                else:
                    act.wait_ge(applied0, r // 2 + 1)
                evacuate3(2, r, r % SLOTS)

            def evacuate3_tile3(r):
                act.wait_ge(added1, r + 1)
                evacuate3(3, r, r % SLOTS)

            for r in range(SLOTS):
                evacuate3_tile2(r)
            square_root(4)
            act.wait_ge(bn_ready, 4)
            for r in range(SLOTS, R):
                scale_tile(1, SCALAR_PAIRS[r - SLOTS], scaled1)
                evacuate3_tile2(r)

            for r in range(SLOTS):
                if r + SLOTS < len(SCALAR_PAIRS):
                    scale_tile(1, SCALAR_PAIRS[r + SLOTS], scaled1)
                evacuate3_tile3(r)
                if r == 0:
                    square_root(5)
            for r in range(SLOTS, R - 1):
                evacuate3_tile3(r)
            for c in range(3):
                if c == 2:
                    square_root(6)
                    evacuate3_tile3(R - 1)
                    act.wait_ge(tile2_applied, 1)
                else:
                    act.wait_ge(added0 if c == 0 else added1, 1)
                nc.scalar.activation(x[:, 0, c, :], x[:, 0, c, :], ACT.Relu, bias=shift3[:, c:c + 1]).then_inc(x1_relu, 1)
                act.wait_ge(x1_relu, c + 1)
                if c == 0:
                    act.wait_ge(conv3_done, CT * R)
                nc.scalar.activation(xs1[0][0][:, c, :], x[:, 0, c, :], ACT.Copy).then_inc(first_h, 1)

            def second_relu(c):
                nc.scalar.activation(x[:, 1, c, :], x[:, 1, c, :], ACT.Relu, bias=shift3[:, c:c + 1]).then_inc(x1_relu, 1)

            second_relu(0)

            def split_high1(g, s):
                act.wait_ge(x1_ready, g)
                need(act, bconv1_done, g - 1)
                nc.scalar.activation(xs1[s][0][:, :, :], xg(g), ACT.Copy).then_inc(x1h_ready, 1)

            def t1_high(g, s):
                act.wait_ge(bconv1_done, g + 1)
                need(act, bconv2_done, g - 1)
                nc.scalar.activation(t1[s][0][:, :], ps[:, s, 0:N], ACT.Identity, bias=bias_t1[:, 0:1]).then_inc(t1h_ready, 1)

            def t2_high(g, s):
                act.wait_ge(bconv2_done, g + 1)
                need(act, bconv3_done, g - 1)
                nc.scalar.activation(t2[s][0][:, :], ps[:, 2 + s, 0:N], ACT.Identity, bias=bias_t2[:, 0:1]).then_inc(t2h_ready, 1)

            def finish(g):
                act.wait_ge(sum_ready, g + 1)
                nc.scalar.activation(xg(g), xg(g), ACT.Relu, bias=bias_y[:, 0:1]).then_inc(y_ready, 1)

            act.wait_ge(x1_first, 1)
            nc.scalar.activation(xs1[0][0][:, 3, :], x[:, 0, 3, :], ACT.Copy).then_inc(last_h, 1)
            second_relu(1)
            t1_high(0, 0)
            split_high1(1, 1)
            t2_high(0, 0)
            t1_high(1, 1)
            split_high1(2, 0)
            finish(0)
            t2_high(1, 1)
            with act.Fori(1, (G - 2) // 2) as r:
                for s in range(2):
                    g = r * 2 + s
                    t1_high(g, s)
                    split_high1(g + 1, 1 - s)
                    finish(g - 1)
                    t2_high(g, s)
            t1_high(G - 2, 0)
            split_high1(G - 1, 1)
            finish(G - 3)
            t2_high(G - 2, 0)
            t1_high(G - 1, 1)
            finish(G - 2)
            t2_high(G - 1, 1)
            for c in range(CT):
                act.wait_ge(last_sum, c + 1)
                nc.scalar.activation(x[:, G - 1, c, :], x[:, G - 1, c, :], ACT.Relu, bias=bias_y[:, 0:1]).then_inc(y_ready, 1)

        @block.vector
        def _(dve):
            steps = [0]

            def chain(instruction):
                steps[0] += 1
                instruction.then_inc(dve_done, 1)
                dve.wait_ge(dve_done, steps[0])

            nc.vector.memset(warm[:, :], 0.0).then_inc(warm_ready, 1)
            nc.vector.memset(one[:, :], 1.0).then_inc(one_ready, 1)
            dve.wait_ge(w1h_ready, 1)
            nc.vector.tensor_tensor(wl[:, 0:CT], stage[:, 0:CT], wh[:, 0:CT].bitcast(F32), ALU.subtract).then_inc(w1l_ready, 1)

            def split_low(g, s):
                dve.wait_ge(xh_ready, g)
                nc.vector.tensor_tensor(xs0[s][1][:, 0:CT - 1, :], xg(g)[:, 0:CT - 1, :], xs0[s][0][:, 0:CT - 1, :].bitcast(F32),
                                        ALU.subtract).then_inc(xl_ready, 1)

            def gather(half, g, y, ready, count):
                dve.wait_ge(ready, count)
                nc.vector.bn_stats(stats[:, half, bass.ds(g, 1), :].rearrange("p a n -> p (a n)"), y).then_inc(stats_done, 1)

            for c in range(CT):
                dve.wait_ge(x0h_ready, c + 1)
                nc.vector.tensor_tensor(xs0[0][1][:, c, :], x[:, 0, c, :], xs0[0][0][:, c, :].bitcast(F32), ALU.subtract).then_inc(x0l_ready, 1)
            dve.wait_ge(par_loaded, 32)
            for i, c in enumerate((G1, G2)):
                nc.vector.tensor_scalar(half_g[:, i:i + 1], par[:, c:c + 1], -0.5, None, ALU.mult).then_inc(half_ready, 1)
            split_low(1, 1)
            for g in range(XS - 2):
                split_low(g + 2, g + 2)
                gather(0, g, y3g(0, g), y1_ready, g + 1)
            with dve.Fori(1, G // XS - 1) as r:
                for s in range(XS):
                    split_low(r * XS + s, s)
                    gather(0, r * XS + s - 2, y3g(0, r * XS + s - 2), y1_ready, r * XS + s - 1)
            for s in range(XS - 1):
                split_low(G - XS + s, s)
                gather(0, G - XS + s - 2, y3g(0, G - XS + s - 2), y1_ready, G - XS + s - 1)
            for c in range(CT):
                dve.wait_ge(x15h_ready, c + 1)
                nc.vector.tensor_tensor(xs0[XS - 1][1][:, c, :], x[:, G - 1, c, :], xs0[XS - 1][0][:, c, :].bitcast(F32),
                                        ALU.subtract).then_inc(x15l_ready, 1)
            for g in range(G - 3, G - 1):
                gather(0, g, y3g(0, g), y1_ready, g + 1)
            gather(0, G - 1, ps[:, XS - 1, 0:N], conv1_done, G)

            def batch_norm(n, buffer, bias, half_gamma, beta, scale, shift, meanwhile=None):
                meanwhile = meanwhile or (lambda k: None)
                chain(nc.vector.bn_aggr(mv[:, :], stats[:, buffer].rearrange("p g s -> p (g s)")))
                nc.vector.tensor_scalar(var_eps[:, :], mv[:, 1:2], EPS, None, ALU.add).then_inc(var_ready, 1)
                nc.vector.scalar_tensor_tensor(mean_off[:, :], mv[:, 0:1], bias, bias, ALU.add, ALU.subtract).then_inc(mean_ready, 1)
                meanwhile(0)
                meanwhile(1)
                dve.wait_ge(std_ready, n)
                chain(nc.vector.reciprocal(r0[:, :], std[:, :]))
                nc.vector.tensor_tensor(gr[:, :], r0[:, :], half_gamma, ALU.mult)
                last = nc.vector.scalar_tensor_tensor(vrr[:, :], r0[:, :], var_eps[:, :], r0[:, :], ALU.mult, ALU.mult)
                steps[0] += 1
                last.then_inc(dve_done, 1)
                meanwhile(2)
                dve.wait_ge(dve_done, steps[0])
                last = nc.vector.scalar_tensor_tensor(scale, vrr[:, :], -3.0, gr[:, :], ALU.add, ALU.mult)
                steps[0] += 1
                last.then_inc(dve_done, 1)
                meanwhile(3)
                dve.wait_ge(dve_done, steps[0])
                dve.wait_ge(mean_ready, n)
                nc.vector.scalar_tensor_tensor(shift, mean_off[:, :], scale, beta, ALU.mult, ALU.subtract, reverse1=True).then_inc(bn_ready, 1)
                dve.wait_ge(bn_ready, n)

            def col(c, w=1):
                return par[:, c:c + w]

            dve.wait_ge(half_ready, 2)
            dve.wait_ge(stats_done, G)
            batch_norm(1, 0, col(B1), half_g[:, 0:1], col(BE1), scale1[:, :], shift1[:, :])

            def split1(g, s):
                need(dve, conv2_done, g - 1)
                dve.wait_ge(a1_ready, g + 1)
                nc.vector.tensor_scalar(t1[s][0][:, :], y3g(0, g), 1.0, None, ALU.mult).then_inc(a1h_ready, 1)
                dve.wait_ge(a1h_ready, g + 1)
                nc.vector.tensor_tensor(t1[s][1][:, :], y3g(0, g), t1[s][0][:, :].bitcast(F32), ALU.subtract).then_inc(a1l_ready, 1)

            split1(0, 0)
            split1(1, 1)
            s_ = scal[:, RES_SCALE:RES_SCALE + 1]
            nc.vector.scalar_tensor_tensor(sp[:, 0:1], s_, -1.0, s_, ALU.mult, ALU.max).then_inc(sp_ready, 1)
            dve.wait_ge(sp_exp, 1)
            nc.vector.tensor_scalar(sp[:, 2:3], sp[:, 1:2], 1.0, None, ALU.add).then_inc(sp_ready, 1)
            dve.wait_ge(sp_ready, 2)
            chain(nc.vector.tensor_scalar(sp[:, 4:5], sp[:, 2:3], -1.0, TINY, ALU.add, ALU.add))
            chain(nc.vector.reciprocal(sp[:, 5:6], sp[:, 4:5]))
            dve.wait_ge(sp_log, 1)
            chain(nc.vector.scalar_tensor_tensor(sp[:, 6:7], sp[:, 3:4], TINY, sp[:, 5:6], ALU.add, ALU.mult))
            chain(nc.vector.tensor_tensor(sp[:, 4:5], sp[:, 6:7], sp[:, 1:2], ALU.mult))
            chain(nc.vector.scalar_tensor_tensor(sp[:, 7:8], s_, 0.0, sp[:, 4:5], ALU.max, ALU.add))
            nc.vector.tensor_scalar(g3s[:, :], par[:, G3:G3 + CT], sp[:, 7:8], None, ALU.mult)
            chain(nc.vector.tensor_scalar(be3s[:, :], par[:, BE3:BE3 + CT], sp[:, 7:8], None, ALU.mult))
            chain(nc.vector.tensor_scalar(half_g[:, 2:2 + CT], g3s[:, :], -0.5, None, ALU.mult))

            def sc(c):
                return scal[:, c:c + 1]
            nc.vector.tensor_tensor(bias_t1[:, :], sc(BIAS1B), sc(BIAS2A), ALU.add)
            nc.vector.tensor_tensor(bias_t2[:, :], sc(BIAS2B), sc(BIAS3A), ALU.add)
            chain(nc.vector.scalar_tensor_tensor(bias_y[:, :], sc(BIAS3B), sc(RSCALE), sc(RBIAS), ALU.mult, ALU.add))

            gather(0, 0, a2g(0), y2_ready, 1)
            with dve.Fori(1, G // 2) as r:
                for s in range(2):
                    split1(r * 2 + s, s)
                    gather(0, r * 2 + s - 1, a2g(r * 2 + s - 1), y2_ready, r * 2 + s)
            gather(0, G - 1, ps[:, (G - 1) % 2, 0:N], conv2_done, G)
            dve.wait_ge(stats_done, 2 * G)
            batch_norm(2, 0, col(B2), half_g[:, 1:2], col(BE2), scale2[:, :], shift2[:, :])

            def gather3(tile, r, i):
                if i == 0:
                    dve.wait_ge(y3_ready, tile * R + r + 1)
                g = r * 2 + i
                nc.vector.bn_stats(stats[:, tile % 2, bass.ds(g, 1), :].rearrange("p a n -> p (a n)"), y3g(tile % 2, g)).then_inc(stats_done, 1)

            def norm3(tile, meanwhile=None):
                dve.wait_ge(stats_done, (3 + tile) * G)
                batch_norm(3 + tile, tile % 2, col(B3 + tile), half_g[:, 2 + tile:3 + tile], be3s[:, tile:tile + 1],
                           scale3[:, tile:tile + 1], shift3[:, tile:tile + 1], meanwhile)

            def apply(g, c):
                return nc.vector.scalar_tensor_tensor(xt(g, c), y3g(c % 2, g), scale3[:, c:c + 1], xt(g, c), ALU.mult, ALU.add)

            def apply_tile0(r):
                nc.vector.scalar_tensor_tensor(xp(r, 0), y3p(0, r), scale3[:, 0:1], xp(r, 0), ALU.mult, ALU.add).then_inc(applied0, 1)

            for r in (1, 2):
                nc.vector.tensor_scalar(a2[:, 2 * r:2 * r + 2, :], a2[:, 2 * r:2 * r + 2, :], scale2[:, 0:1], shift2[:, 0:1],
                                        ALU.mult, ALU.add).then_inc(a2_scaled, 1)
                dve.wait_ge(a2_scaled, r)
                nc.vector.tensor_scalar(a2[:, 2 * r:2 * r + 2, :], a2[:, 2 * r:2 * r + 2, :], 0.0, None, ALU.max).then_inc(a2b_ready, 1)
            with dve.Fori(0, R // 4) as k:
                for j in range(4):
                    for i in range(2):
                        gather3(0, k * 4 + j, i)
            norm3(0, lambda k: gather3(1, k // 2, k % 2))
            apply_tile0(1)
            with dve.Fori(1, R // 2) as k:
                for j in range(2):
                    for i in range(2):
                        gather3(1, k * 2 + j, i)
                apply_tile0(k * 2 + 1)
            norm3(1, lambda k: gather3(2, k // 2, k % 2))
            for r in range(2, R):
                for i in range(2):
                    gather3(2, r, i)
                if r + 1 in VECTOR_PAIRS:
                    nc.vector.tensor_scalar(y3p(1, r + 1), y3p(1, r + 1), scale3[:, 1:2], None, ALU.mult).then_inc(vector_scaled1, 1)
            norm3(2, lambda k: gather3(3, k // 2, k % 2))
            for r in range(2, R - 1):
                for i in range(2):
                    gather3(3, r, i)
            dve.wait_ge(conv3_done, CT * R)
            for g in (G - 2, G - 1):
                nc.vector.bn_stats(stats[:, 1, g, :], ps[:, BANKS - G + g, 0:N]).then_inc(stats_done, 1)
            norm3(3, lambda k: apply(0, 2).then_inc(tile2_applied, 1) if k == 0 else None)

            def shift_relu(g, c):
                return nc.vector.tensor_scalar(xt(g, c), xt(g, c), shift3[:, c:c + 1], 0.0, ALU.add, ALU.max)

            def block0_sum(g):
                apply(g, 2)
                apply(g, 3).then_inc(x1_part, 1)
                shift_relu(g, 0)

            def block0_relu(g):
                shift_relu(g, 1)
                dve.wait_ge(x1_part, g - 1)
                shift_relu(g, 2)
                shift_relu(g, 3).then_inc(x1_ready, 1)

            def split_low1(g, s):
                dve.wait_ge(x1h_ready, g)
                nc.vector.tensor_tensor(xs1[s][1][:, :, :], xg(g), xs1[s][0][:, :, :].bitcast(F32), ALU.subtract).then_inc(x1l_ready, 1)

            def t1_low(g, s):
                dve.wait_ge(t1h_ready, g + 1)
                nc.vector.scalar_tensor_tensor(t1[s][1][:, :], ps[:, s, 0:N], bias_t1[:, 0:1], t1[s][0][:, :].bitcast(F32),
                                               ALU.add, ALU.subtract).then_inc(t1l_ready, 1)

            def t2_low(g, s):
                dve.wait_ge(t2h_ready, g + 1)
                nc.vector.scalar_tensor_tensor(t2[s][1][:, :], ps[:, 2 + s, 0:N], bias_t2[:, 0:1], t2[s][0][:, :].bitcast(F32),
                                               ALU.add, ALU.subtract).then_inc(t2l_ready, 1)

            def add_result(g):
                dve.wait_ge(bconv3_done, g + 1)
                nc.vector.scalar_tensor_tensor(xg(g), ps[:, 4:8, 0:N], scal[:, RSCALE:RSCALE + 1], xg(g),
                                               ALU.mult, ALU.add).then_inc(sum_ready, 1)

            chain(apply(0, 3))
            nc.vector.tensor_scalar(xt(0, 3), xt(0, 3), shift3[:, 3:4], 0.0, ALU.add, ALU.max).then_inc(x1_first, 1)
            dve.wait_ge(last_h, 1)
            nc.vector.tensor_tensor(xs1[0][1][:, 3, :], x[:, 0, 3, :], xs1[0][0][:, 3, :].bitcast(F32), ALU.subtract).then_inc(last_l, 1)
            dve.wait_ge(y3_ready, CT * R)
            dve.wait_ge(added0, R // 2)
            dve.wait_ge(added1, R)
            apply(1, 2)
            chain(apply(1, 3))
            dve.wait_ge(x1_relu, 5)
            shift_relu(1, 2)
            t1_low(0, 0)
            shift_relu(1, 3).then_inc(x1_ready, 1)
            split_low1(1, 1)
            block0_sum(2)
            t2_low(0, 0)
            block0_relu(2)
            t1_low(1, 1)
            add_result(0)
            split_low1(2, 0)
            block0_sum(3)
            t2_low(1, 1)
            block0_relu(3)
            with dve.Fori(1, (G - 2) // 2) as r:
                for s in range(2):
                    g = r * 2 + s
                    t1_low(g, s)
                    add_result(g - 1)
                    split_low1(g + 1, 1 - s)
                    block0_sum(g + 2)
                    t2_low(g, s)
                    block0_relu(g + 2)
            t1_low(G - 2, 0)
            add_result(G - 3)
            split_low1(G - 1, 1)
            t2_low(G - 2, 0)
            t1_low(G - 1, 1)
            add_result(G - 2)
            t2_low(G - 1, 1)
            for c in range(CT):
                dve.wait_ge(bconv3_done, G + c)
                nc.vector.scalar_tensor_tensor(x[:, G - 1, c, :], ps[:, 4 + c, 0:N], scal[:, RSCALE:RSCALE + 1], x[:, G - 1, c, :],
                                               ALU.mult, ALU.add).then_inc(last_sum, 1)

        @block.tensor
        def _(pe):
            def products(bank, terms):
                passes = [p for t, vh, vl in terms for p in ((wh, t, vh), (wh, t, vl), (wl, t, vh))]
                for i, (w, t, v) in enumerate(passes):
                    last = nc.tensor.matmul(ps[:, bank, 0:N], w[:, t, :], v, start=i == 0, stop=i == len(passes) - 1)
                return last

            def in_image(shift, size):
                return slice(max(-shift, 0), size - max(shift, 0)), slice(max(shift, 0), size - max(-shift, 0))

            def conv_1x1(bank, split):
                return products(bank, [(W1 + c, split[0][:, c, :], split[1][:, c, :]) for c in range(CT)])

            def tap(bank, k, w, v, start, stop):
                (rows_out, rows_in), (cols_out, cols_in) = in_image(k // 3 - 1, H), in_image(GI * (k % 3 - 1), GI * W)
                return nc.tensor.matmul(rows(ps[:, bank, 0:N])[:, rows_out, cols_out], w[:, W2 + k, :], rows(v[:, :])[:, rows_in, cols_in],
                                        start=start, stop=stop)

            TAP_ORDER = sorted(range(TAPS), key=lambda k: k != TAPS // 2)

            def conv_3x3(bank, split):
                h, l = split
                for i, k in enumerate(TAP_ORDER):
                    for j, (w, v) in enumerate(((wh, h), (wh, l), (wl, h))):
                        last = tap(bank, k, w, v, i + j == 0, i == TAPS - 1 and j == 2)
                return last

            def conv_3x3_first(bank, split, high_ready, low_ready):
                pe.wait_ge(high_ready, 1)
                for i, k in enumerate(TAP_ORDER):
                    for w in (wh, wl):
                        tap(bank, k, w, split[0], i == 0 and w is wh, False)
                pe.wait_ge(low_ready, 1)
                for k in TAP_ORDER:
                    last = tap(bank, k, wh, split[1], False, k == TAP_ORDER[-1])
                return last

            def conv1(g, s):
                pe.wait_ge(xl_ready, g)
                pe.wait_ge(xl3_ready, g)
                need(pe, y1_ready, g - XS + 1)
                conv_1x1(s, xs0[s]).then_inc(conv1_done, 1)

            def products_1x1_by_tile(bank, split, ready, fill=(0,) * CT, last_high=None):
                for c in range(CT):
                    keep_warm(fill[c], 1)
                    if c == CT - 1 and last_high:
                        pe.wait_ge(*last_high)
                    else:
                        pe.wait_ge(*ready[c])
                    h, l = split[0][:, c, :], split[1][:, c, :]
                    for i, (w, v) in enumerate(((wh, h), (wl, h), (wh, l))):
                        if c == CT - 1 and last_high and i == 2:
                            pe.wait_ge(*ready[c])
                        last = nc.tensor.matmul(ps[:, bank, 0:N], w[:, W1 + c, :], v, start=c + i == 0, stop=c == CT - 1 and i == 2)
                return last

            def keep_warm(count, bank=BANKS - 1):
                for i in range(count):
                    nc.tensor.matmul(ps[:, bank, 0:N], warm[:, 0:P], warm[:, :], start=True, stop=True)

            pe.wait_ge(warm_ready, 1)
            keep_warm(10)
            pe.wait_ge(w1l_ready, 1)
            products_1x1_by_tile(0, xs0[0], [(x0l_ready, c + 1) for c in range(CT)]).then_inc(conv1_done, 1)
            for s in range(1, XS):
                conv1(s, s)
            with pe.Fori(1, G // XS - 1) as r:
                for s in range(XS):
                    conv1(r * XS + s, s)
            for s in range(XS - 1):
                conv1(G - XS + s, s)
            pe.wait_ge(y1_ready, G - XS)
            products_1x1_by_tile(XS - 1, xs0[XS - 1], [(x15l_ready, c + 1) for c in range(CT)]).then_inc(conv1_done, 1)
            keep_warm(28)

            def conv2(g, s):
                pe.wait_ge(a1l_ready, g + 1)
                need(pe, y2_ready, g - 1)
                conv_3x3(s, t1[s]).then_inc(conv2_done, 1)

            pe.wait_ge(w2_ready, 1)
            conv_3x3_first(0, t1[0], a1h_ready, a1l_ready).then_inc(conv2_done, 1)
            conv2(1, 1)
            with pe.Fori(1, G // 2) as r:
                for s in range(2):
                    conv2(r * 2 + s, s)

            keep_warm(22)

            def conv3(tile, r, s):
                if tile == 0 and r in (1, 2):
                    pe.wait_ge(a2b_ready, r)
                elif tile == 0:
                    pe.wait_ge(a2_ready, 1 if r == 0 else r - 1)
                need(pe, y3_ready, tile * R + r - SLOTS + 1)
                for i in range(2):
                    last = nc.tensor.matmul(ps[:, 2 * s + i, 0:N], w3s[:, tile, :], a2g(r * 2 + i), start=True, stop=True)
                last.then_inc(conv3_done, 1)

            pe.wait_ge(w03_loaded, 16)
            for s in range(SLOTS):
                conv3(0, s, s)
            for s in range(SLOTS):
                conv3(0, SLOTS + s, s)
            for tile in range(1, CT):
                with pe.Fori(0, R // SLOTS) as k:
                    for s in range(SLOTS):
                        conv3(tile, k * SLOTS + s, s)

            def b_conv1(g, s):
                pe.wait_ge(x1l_ready, g)
                need(pe, t1l_ready, g - 1)
                conv_1x1(s, xs1[s]).then_inc(bconv1_done, 1)

            def b_conv2(g, s):
                pe.wait_ge(t1l_ready, g + 1)
                need(pe, t2l_ready, g - 1)
                conv_3x3(2 + s, t1[s]).then_inc(bconv2_done, 1)

            def b_conv3(g, s):
                pe.wait_ge(t2l_ready, g + 1)
                need(pe, sum_ready, g)
                for c in range(CT):
                    last = products(4 + c, [(W3 + c, t2[s][0][:, :], t2[s][1][:, :])])
                last.then_inc(bconv3_done, 1)

            pe.wait_ge(wb1_ready, 1)
            pe.wait_ge(y3_ready, CT * R - SLOTS + 1)
            products_1x1_by_tile(0, xs1[0], [(first_l, 1), (first_l, 2), (first_l, 3), (last_l, 1)], (12, 0, 12, 2), (last_h, 1)).then_inc(bconv1_done, 1)
            conv_3x3_first(2, t1[0], t1h_ready, t1l_ready).then_inc(bconv2_done, 1)
            pe.wait_ge(wb1c_ready, 1)
            b_conv1(1, 1)
            b_conv3(0, 0)
            b_conv2(1, 1)
            with pe.Fori(1, G // 2) as r:
                for s in range(2):
                    g = r * 2 + s
                    b_conv1(g, s)
                    b_conv3(g - 1, 1 - s)
                    b_conv2(g, s)
            pe.wait_ge(t2l_ready, G)
            pe.wait_ge(sum_ready, G - 1)
            for c in range(CT):
                products(4 + c, [(W3 + c, t2[1][0][:, :], t2[1][1][:, :])]).then_inc(bconv3_done, 1)


def kernel(x, L0_conv_w1, L0_conv_b1, L0_conv_g1, L0_conv_be1, L0_conv_w2, L0_conv_b2, L0_conv_g2, L0_conv_be2,
           L0_conv_w3, L0_conv_b3, L0_conv_g3, L0_conv_be3, L0_conv_residual_scale, L1_conv_w1, L1_conv_w2,
           L1_conv_w3, L1_conv_bias1b, L1_conv_bias2a, L1_conv_bias2b, L1_conv_bias3a, L1_conv_bias3b,
           L1_conv_rscale, L1_conv_rbias):
    import numpy as np
    import concourse.bacc as bacc
    from concourse.bass_utils import run_bass_kernel_spmd

    def weights(w1, w2, w3):
        a = np.asarray(w1).reshape(P, CT, P).transpose(2, 1, 0)
        b = np.asarray(w2).reshape(P, P, TAPS).transpose(1, 2, 0)
        c = np.asarray(w3).reshape(CT, P, P).transpose(2, 0, 1)
        return np.ascontiguousarray(np.concatenate([a, b, c], axis=1))

    def columns(*vectors):
        return np.ascontiguousarray(np.concatenate([np.asarray(v).reshape(-1, P).T for v in vectors], axis=1))

    arrays = {
        "x_dram": np.ascontiguousarray(np.asarray(x).reshape(G, GI, CT, P, H, W).transpose(3, 0, 2, 4, 5, 1)).reshape(P, G, CT, N),
        "w0_dram": weights(L0_conv_w1, L0_conv_w2, L0_conv_w3),
        "w1_dram": weights(L1_conv_w1, L1_conv_w2, L1_conv_w3),
        "par_dram": columns(L0_conv_b1, L0_conv_g1, L0_conv_be1, L0_conv_b2, L0_conv_g2, L0_conv_be2,
                            L0_conv_b3, L0_conv_g3, L0_conv_be3),
        "scal_dram": np.concatenate([np.asarray(v) for v in (
            L0_conv_residual_scale, L1_conv_rscale, L1_conv_rbias, L1_conv_bias1b, L1_conv_bias2a,
            L1_conv_bias2b, L1_conv_bias3a, L1_conv_bias3b)]),
    }
    nc = bacc.Bacc("TRN2", target_bir_lowering=False, num_devices=1)
    args = [nc.dram_tensor(n, a.shape, mybir.dt.from_np(a.dtype), kind="ExternalInput").ap() for n, a in arrays.items()]
    out = nc.dram_tensor("out_dram", (P, G, CT, N), F32, kind="ExternalOutput").ap()
    build(nc, *args, out)
    r = run_bass_kernel_spmd(nc, [arrays], core_ids=[0])
    y = r.results[0]["out_dram"].reshape(P, G, CT, H, W, GI).transpose(1, 5, 2, 0, 3, 4)
    return np.ascontiguousarray(y).reshape(IMAGES, CHANNELS, H, W)
```
